# Optimizing a Trainium2 kernel written in Bass

```python
import numpy as np
import jax
import jax.numpy as jnp

def _softmax(x, axis=-1):
    return jax.nn.softmax(x, axis=axis)

def _gelu(x):
    return jax.nn.gelu(x, approximate=True)

def _silu(x):
    return jax.nn.silu(x)

def _sigmoid(x):
    return jax.nn.sigmoid(x)

def _layernorm(x, axis=-1, eps=1e-05):
    m = jnp.mean(x, axis=axis, keepdims=True)
    v = jnp.var(x, axis=axis, keepdims=True)
    return (x - m) / jnp.sqrt(v + eps)

def _scatter_add(tgt, idx, src, axis=0):
    return tgt.at[idx].add(src)

def _segment_sum(src, seg, n):
    return jax.ops.segment_sum(src, seg, n)
kernel_name = 'mk_recurrent_d1_jaxref_r8_d90832'

def setup_inputs(seed: int=0):
    np.random.seed(seed)
    _w = jnp.asarray

    def _L0_attn_setup():
        import jax, jax.numpy as jnp
        import numpy as np
        HID = 128
        RATIO = 4
        SELECT_K = 64
        WINDOW = 32
        N_HEADS = 16
        SCALE = 1.0 / np.sqrt(HID // N_HEADS)

        def _adjust(t, L):
            cur = t.shape[1]
            if cur < L:
                return jnp.pad(t, ((0, 0), (0, L - cur), (0, 0)))
            return t[:, :L]

        def _attend(x, Wq, bq, Wk, bk, Wv, bv):
            q = x @ Wq + bq
            k = x @ Wk + bk
            v = x @ Wv + bv
            s = jnp.einsum('...qd,...kd->...qk', q, k) * SCALE
            p = jax.nn.softmax(s, axis=-1)
            return jnp.einsum('...qk,...kd->...qd', p, v)
        key = jax.random.key(seed)
        ks = jax.random.split(key, 12)
        std = 0.02
        d = {'hidden_states': jax.random.normal(ks[0], (4, 512, HID), jnp.float32), 'Wq': jax.random.normal(ks[1], (HID, HID), jnp.float32) * std, 'bq': jnp.zeros((HID,), jnp.float32), 'Wk': jax.random.normal(ks[2], (HID, HID), jnp.float32) * std, 'bk': jnp.zeros((HID,), jnp.float32), 'Wv': jax.random.normal(ks[3], (HID, HID), jnp.float32) * std, 'bv': jnp.zeros((HID,), jnp.float32), 'Wo': jax.random.normal(ks[4], (3 * HID, HID), jnp.float32) * std, 'bo': jnp.zeros((HID,), jnp.float32), 'Wg': jax.random.normal(ks[5], (HID, 3), jnp.float32) * std, 'bg': jnp.zeros((3,), jnp.float32), 'Wc': jax.random.normal(ks[6], (RATIO * HID, HID), jnp.float32) * std, 'bc': jnp.zeros((HID,), jnp.float32), 'Ws': jax.random.normal(ks[7], (HID, 1), jnp.float32) * std, 'bs': jnp.zeros((1,), jnp.float32)}
        return d
    _L0_attn_in = _L0_attn_setup()

    def _L0_ffn_setup():
        import jax, jax.numpy as jnp
        import numpy as np
        HEADS = 8
        DIM = 128
        DIM_KEY = 64
        NUM_KEYS = 32
        TOPK = 16
        key = jax.random.key(seed)
        k1, k2, k3, k4, k5 = jax.random.split(key, 5)
        b, n = (4, 256)
        x = jax.random.normal(k1, (b, n, DIM), dtype=jnp.float32)
        Wq = jax.random.normal(k2, (2 * HEADS * DIM_KEY, DIM), dtype=jnp.float32) * 0.02
        keys = jax.random.normal(k3, (HEADS, NUM_KEYS, 2, DIM_KEY), dtype=jnp.float32)
        W_down = jax.random.normal(k4, (8192, DIM), dtype=jnp.float32)
        W_up = jax.random.normal(k5, (8192, DIM), dtype=jnp.float32)
        return {'x': x, 'Wq': Wq, 'keys': keys, 'W_down': W_down, 'W_up': W_up}
    _L0_ffn_in = _L0_ffn_setup()
    _d = {'L0_attn_hidden_states': _L0_attn_in['hidden_states'], 'L0_attn_Wq': _L0_attn_in['Wq'], 'L0_attn_bq': _L0_attn_in['bq'], 'L0_attn_Wk': _L0_attn_in['Wk'], 'L0_attn_bk': _L0_attn_in['bk'], 'L0_attn_Wv': _L0_attn_in['Wv'], 'L0_attn_bv': _L0_attn_in['bv'], 'L0_attn_Wo': _L0_attn_in['Wo'], 'L0_attn_bo': _L0_attn_in['bo'], 'L0_attn_Wg': _L0_attn_in['Wg'], 'L0_attn_bg': _L0_attn_in['bg'], 'L0_attn_Wc': _L0_attn_in['Wc'], 'L0_attn_bc': _L0_attn_in['bc'], 'L0_attn_Ws': _L0_attn_in['Ws'], 'L0_attn_bs': _L0_attn_in['bs'], 'L0_ffn_Wq': _L0_ffn_in['Wq'], 'L0_ffn_keys': _L0_ffn_in['keys'], 'L0_ffn_W_down': _L0_ffn_in['W_down'], 'L0_ffn_W_up': _L0_ffn_in['W_up']}
    _x0 = _d['L0_attn_hidden_states']
    _d['L0_attn_hidden_states'] = jax.random.normal(jax.random.fold_in(jax.random.key(seed), 1), (8, 512, 128), dtype=_x0.dtype)
    del _x0
    return _d

def reference(L0_attn_hidden_states, L0_attn_Wq, L0_attn_bq, L0_attn_Wk, L0_attn_bk, L0_attn_Wv, L0_attn_bv, L0_attn_Wo, L0_attn_bo, L0_attn_Wg, L0_attn_bg, L0_attn_Wc, L0_attn_bc, L0_attn_Ws, L0_attn_bs, L0_ffn_Wq, L0_ffn_keys, L0_ffn_W_down, L0_ffn_W_up):

    def _L0_attn_ref(hidden_states, Wq, bq, Wk, bk, Wv, bv, Wo, bo, Wg, bg, Wc, bc, Ws, bs):
        import jax, jax.numpy as jnp
        import numpy as np
        HID = 128
        RATIO = 4
        SELECT_K = 64
        WINDOW = 32
        N_HEADS = 16
        SCALE = 1.0 / np.sqrt(HID // N_HEADS)

        def _adjust(t, L):
            cur = t.shape[1]
            if cur < L:
                return jnp.pad(t, ((0, 0), (0, L - cur), (0, 0)))
            return t[:, :L]

        def _attend(x, Wq, bq, Wk, bk, Wv, bv):
            q = x @ Wq + bq
            k = x @ Wk + bk
            v = x @ Wv + bv
            s = jnp.einsum('...qd,...kd->...qk', q, k) * SCALE
            p = jax.nn.softmax(s, axis=-1)
            return jnp.einsum('...qk,...kd->...qd', p, v)
        B, L, H = hidden_states.shape
        gates = jax.nn.sigmoid(hidden_states @ Wg + bg)
        gates = gates / (gates.sum(-1, keepdims=True) + 1e-06)
        pad_c = -L % RATIO
        xc = jnp.pad(hidden_states, ((0, 0), (0, pad_c), (0, 0)))
        blocks = xc.reshape(B, -1, RATIO * H)
        compressed = blocks @ Wc + bc
        comp_out = _adjust(_attend(compressed, Wq, bq, Wk, bk, Wv, bv), L)
        k_eff = min(SELECT_K, L)
        scores = (hidden_states @ Ws + bs)[..., 0]
        _, idx = jax.lax.top_k(scores, k_eff)
        idx = jnp.sort(idx, axis=-1)
        selected = jnp.take_along_axis(hidden_states, idx[..., None], axis=1)
        sel_out = _adjust(_attend(selected, Wq, bq, Wk, bk, Wv, bv), L)
        W = min(WINDOW, L)
        pad_w = -L % W
        xw = jnp.pad(hidden_states, ((0, 0), (0, pad_w), (0, 0)))
        Lp = xw.shape[1]
        starts = np.arange(0, Lp - W + 1, W // 2)
        widx = starts[:, None] + np.arange(W)
        win = xw[:, widx]
        win_ctx = _attend(win, Wq, bq, Wk, bk, Wv, bv)
        win_out = _adjust(win_ctx.reshape(B, -1, H), L)
        combined = jnp.concatenate([comp_out * gates[..., 0:1], sel_out * gates[..., 1:2], win_out * gates[..., 2:3]], axis=-1)
        out = combined @ Wo + bo
        out = out * 0.5 + hidden_states * 0.5
        mu = out.mean(-1, keepdims=True)
        var = out.var(-1, keepdims=True)
        return (out - mu) * jax.lax.rsqrt(var + 1e-06)

    def _L0_ffn_ref(x, Wq, keys, W_down, W_up):
        import jax, jax.numpy as jnp
        import numpy as np
        HEADS = 8
        DIM = 128
        DIM_KEY = 64
        NUM_KEYS = 32
        TOPK = 16
        b, n, d = x.shape
        q = (x @ Wq.T).reshape(b, n, 2, HEADS, DIM_KEY).transpose(2, 0, 1, 3, 4)
        sim = jnp.einsum('pbnhd,hkpd->pbnhk', q, keys)
        sx, ix = jax.lax.top_k(sim[0], TOPK)
        sy, iy = jax.lax.top_k(sim[1], TOPK)
        all_scores = (sx[..., :, None] + sy[..., None, :]).reshape(b, n, HEADS, TOPK * TOPK)
        scores, pk_indices = jax.lax.top_k(all_scores, TOPK)
        wd = W_down[pk_indices]
        wu = W_up[pk_indices]
        h = jnp.einsum('bnd,bnhkd->bnhk', x, wd)
        h = jax.nn.gelu(h, approximate=False)
        h = h * jax.nn.softmax(scores, axis=-1)
        return jnp.einsum('bnhk,bnhkd->bnd', h, wu)
    x = L0_attn_hidden_states
    xn = _layernorm(x, axis=-1)
    s = _L0_attn_ref(xn, L0_attn_Wq, L0_attn_bq, L0_attn_Wk, L0_attn_bk, L0_attn_Wv, L0_attn_bv, L0_attn_Wo, L0_attn_bo, L0_attn_Wg, L0_attn_bg, L0_attn_Wc, L0_attn_bc, L0_attn_Ws, L0_attn_bs)
    g = _silu(_L0_ffn_ref(xn, L0_ffn_Wq, L0_ffn_keys, L0_ffn_W_down, L0_ffn_W_up))
    x = x + s * g
    return x

_drawn_inputs = setup_inputs


def setup_inputs(seed=0):
    import zlib

    import numpy as np

    out = dict(_drawn_inputs(seed))
    spreads = {'L0_attn_bq': (0.0, 0.8),
     'L0_attn_bk': (0.0, 0.8),
     'L0_attn_bv': (0.0, 0.8),
     'L0_attn_bo': (0.0, 0.1),
     'L0_attn_bg': (0.0, 0.8),
     'L0_attn_bc': (0.0, 0.8)}
    factors = {'L0_attn_Wq': 8.0,
     'L0_attn_Wk': 8.0,
     'L0_attn_Wv': 8.0,
     'L0_attn_Wo': 6.203,
     'L0_attn_Wg': 8.0,
     'L0_attn_Wc': 8.0,
     'L0_attn_Ws': 8.0}
    for name, (base, spread) in spreads.items():
        noise = np.random.default_rng([zlib.crc32(name.encode()), seed]).standard_normal(out[name].shape)
        drawn = base * np.exp(spread * noise) if base else spread * noise
        out[name] = jnp.asarray(drawn.astype(out[name].dtype))
    for name, factor in factors.items():
        out[name] = (out[name] * factor).astype(out[name].dtype)
    return out
```

```python
from contextlib import ExitStack

import concourse.bass as bass
from concourse import mybir
from concourse.alu_op_type import AluOpType as ALU

F32 = mybir.dt.float32
ACT = mybir.ActivationFunctionType
AX_X = mybir.AxisListType.X

P = 128
RATIO = 4
SELECT_K = 64
WINDOW = 32
STEP_W = WINDOW // 2
N_HEADS = 16
COMP, SEL, WIN = range(3)
HEADS = 8
KEYS = 32
DKEY = 64
TOPK = 16
VECS = 2 * HEADS
ROW_LEN = [TOPK // (i + 1) for i in range(TOPK)]
CANDS = sum(ROW_LEN)
RUNS = []
_at = 0
for _i, _n in enumerate(ROW_LEN):
    if RUNS and RUNS[-1][2] == _n:
        RUNS[-1][1] += 1
    else:
        RUNS.append([_i, 1, _n, _at])
    _at += _n
TAKEN = -1e30
NO_SCORE = -3.3e38
HALF_V = VECS // 2
HALF_H = HEADS // 2


def program(nc, x, wq, bq, wk, bk, wv, bv, wo, bo, wg, bg, wc, bc, ws, bs,
            ffn_wq, ffn_keys, ffn_down, ffn_up, out):
    B, L, D = x.shape
    assert D == P and L % P == 0 and B % 2 == 0
    TB = L // P
    TILES = B * TB
    BLOCKS = L // RATIO
    WPT = P // WINDOW
    WKEYS = STEP_W * (WPT - 1) + WINDOW
    WTOK = STEP_W * WPT * (TB - 1) + WKEYS
    CS = BLOCKS + SELECT_K
    SCALE = float((D // N_HEADS) ** -0.5)
    HK = HEADS * KEYS
    assert TB == 4 and BLOCKS == P and TB * WKEYS + CS <= 512 and 2 * HK <= 512

    ctx = ExitStack()
    with ctx:
        def sb(name, shape, dt=F32):
            return ctx.enter_context(nc.sbuf_tensor(name, shape, dt))

        def bank(name):
            return ctx.enter_context(nc.psum_tensor(name, [P, 512], F32))

        def sem(name):
            return ctx.enter_context(nc.semaphore(name))

        sim_bank = [bank(f"sim{i}") for i in range(2)]
        scratch = [bank(f"scratch{i}") for i in range(2)]
        s_bank = bank("s_bank")
        out_bank = bank("out_bank")
        c_bank = bank("c_bank")
        f_bank = bank("f_bank")

        ident = sb("ident", [P, P])
        ones_row = sb("ones_row", [1, P])
        rank_row = sb("rank_row", [P, SELECT_K])
        neg_half = sb("neg_half", [P, TB])
        win_mask = sb("win_mask", [P, WKEYS])
        wq_sb, wk_sb, wv_sb = (sb(n, [P, D]) for n in ("wq_sb", "wk_sb", "wv_sb"))
        wc_sb = sb("wc_sb", [P, RATIO, D])
        wo_sb = sb("wo_sb", [P, 3, D])
        wz_sb = sb("wz_sb", [P, 4])
        bq_sb, bqs_sb, bk_sb, bv_sb, bc_sb = (sb(n, [P, 1]) for n in ("bq_sb", "bqs_sb", "bk_sb", "bv_sb", "bc_sb"))
        bz_sb = sb("bz_sb", [4, 1])
        bo_row = sb("bo_row", [1, D])
        fwq_sb = sb("fwq_sb", [P, HEADS, D])
        keys_sb = sb("keys_sb", [P, 2, P])
        keysT = sb("keysT", [P, HK])
        sim_w = sb("sim_w", [P, VECS * KEYS])
        down_sb = sb("down_sb", [CANDS, D])
        downT = sb("downT", [P, CANDS])
        up_sb = sb("up_sb", [CANDS, D])

        x_sb = sb("x_sb", [P, TILES, D])
        xn_all = sb("xn_all", [P, TILES, D])
        xT_all = sb("xT_all", [P, TILES * P])
        xns = [sb(f"xns{i}", [P, TB, D]) for i in range(2)]
        xTc = sb("xTc", [P, TB, P])
        st1 = sb("st1", [P, TB, 6])
        mv1 = [sb(f"mv1_{i}", [P, TB, 2]) for i in range(2)]
        rstd1 = [sb(f"rstd1_{i}", [P, TB]) for i in range(2)]
        geluT = sb("geluT", [CANDS, TILES * P])
        zs = [sb(f"zs{i}", [4, L]) for i in range(2)]
        zrow = sb("zrow", [1, TILES * P])
        zg = sb("zg", [P, TILES, 4])
        gexp = sb("gexp", [P, TILES, 3])
        gsig = sb("gsig", [P, TILES, 3])
        gsum = sb("gsum", [P, TILES])
        gates = sb("gates", [P, TILES, 3])

        sc8 = sb("sc8", [B, L])
        sel_a = sb("sel_a", [B, L])
        sel_b = sb("sel_b", [B, L])
        sel_m = sb("sel_m", [B, 8])
        sel_mask = sb("sel_mask", [B, L])
        sel_cnt = sb("sel_cnt", [B, L])
        sel_rank = sb("sel_rank", [B, L])
        zero_row = sb("zero_row", [B, L])
        rank32 = sb("rank32", [TILES, P])
        rankT = sb("rankT", [P, TILES])
        pick = sb("pick", [P, TB, SELECT_K])

        qw = sb("qw", [P, L])
        kw, vw = (sb(n, [P, WTOK]) for n in ("kw", "vw"))
        xsel = sb("xsel", [SELECT_K, D])
        csT = sb("csT", [P, CS])
        qcs, kcs, vcs = (sb(n, [P, CS]) for n in ("qcs", "kcs", "vcs"))
        vww = sb("vww", [WKEYS, TB, D])
        vwc = sb("vwc", [P, 2, D])
        s_win = sb("s_win", [P, TB, WKEYS])
        nmax = sb("nmax", [P, 6])
        rsum = sb("rsum", [P, 6])
        rinv = sb("rinv", [P, 6])
        rgate = sb("rgate", [P, 6])
        p_win = sb("p_win", [P, TB, WKEYS])
        p_cs = sb("p_cs", [P, CS])
        pT_win = sb("pT_win", [WKEYS, TB, P])
        pT_cs = sb("pT_cs", [P, 2, P])
        st2 = sb("st2", [P, TB, 6])
        mv2 = sb("mv2", [P, TB, 2])
        var2 = sb("var2", [P, TB])
        rstd2 = sb("rstd2", [P, TB])
        prod2 = sb("prod2", [P, TB])
        nmr2 = sb("nmr2", [P, TB])
        s_norm = sb("s_norm", [P, TB, D])

        top = [sb(f"top{i}", [P, VECS, TOPK]) for i in range(2)]
        rest = sb("rest", [P, VECS, KEYS])
        shifted = sb("shifted", [P, VECS, TOPK])
        cand = [sb(f"cand{i}", [P, HEADS, CANDS]) for i in range(2)]
        crest = sb("crest", [P, HEADS, CANDS])
        left = [sb(f"left{i}", [P, HEADS, CANDS]) for i in range(2)]
        best = [sb(f"best{i}", [P, HEADS, TOPK]) for i in range(2)]
        e_best = [sb(f"e_best{i}", [P, HEADS, TOPK]) for i in range(2)]
        e_all = [sb(f"e_all{i}", [P, HEADS, CANDS]) for i in range(2)]
        e_left = [sb(f"e_left{i}", [P, HEADS, CANDS]) for i in range(2)]
        den = sb("den", [P, HEADS])
        rden = [sb(f"rden{i}", [P, HEADS]) for i in range(2)]
        prob = sb("prob", [P, HEADS, CANDS])
        wgt = [sb(f"wgt{i}", [P, HEADS, CANDS]) for i in range(2)]
        c_sb = sb("c_sb", [CANDS, L])
        actT = sb("actT", [CANDS, L])
        tanh_f = sb("tanh_f", [P, TB, D])
        half_f = sb("half_f", [P, TB, D])
        y1 = sb("y1", [P, TB, D])
        y2 = sb("y2", [P, TB, D])
        y3 = sb("y3", [P, TB, D])
        y_sb = sb("y_sb", [P, TB, D])

        x_first, x_rest = sem("x_first"), sem("x_rest")
        w_ffn, w_att, w_late = sem("w_ffn"), sem("w_att"), sem("w_late")
        consts = sem("consts")
        prep_pe, prep_dve = sem("prep_pe"), sem("prep_dve")
        stats1, mean1, rstd1_done, xn_done = sem("stats1"), sem("mean1"), sem("rstd1_done"), sem("xn_done")
        pool_step = sem("pool_step")
        xn_stored = [sem(f"xn_stored{i}") for i in range(2)]
        z_stored = [sem(f"z_stored{i}") for i in range(2)]
        sc8_in = sem("sc8_in")
        unit_full, unit_out = sem("unit_full"), sem("unit_out")
        tile_in = [sem(f"tile_in{j}") for j in range(TB)]
        sim_ready, sim_top8, sim_used, top_done = sem("sim_ready"), sem("sim_top8"), sem("sim_used"), sem("top_done")
        shift_done, cand_ready = sem("shift_done"), sem("cand_ready")
        best8, best8_out, best_done, left_done = sem("best8"), sem("best8_out"), sem("best_done"), sem("left_done")
        exp_best, exp_done, den_done, rden_done = sem("exp_best"), sem("exp_done"), sem("den_done"), sem("rden_done")
        prob_done, wgt_done, c_ready, c_out = sem("prob_done"), sem("wgt_done"), sem("c_ready"), sem("c_out")
        act_done, f_ready, f_out = sem("act_done"), sem("f_ready"), sem("f_out")
        sel_step, rank_out, rankT_ready, rankT_out, pick_done = (
            sem(n) for n in ("sel_step", "rank_out", "rankT_ready", "rankT_out", "pick_done"))
        gate_exp, gate_step = sem("gate_exp"), sem("gate_step")
        s_ready, s_masked, max_done, p_exp, rinv_done, rgate_done, p_scaled = (
            sem(n) for n in ("s_ready", "s_masked", "max_done", "p_exp", "rinv_done", "rgate_done", "p_scaled"))
        out_ready, stats2, mean2, norm2_ready, s_done = (
            sem(n) for n in ("out_ready", "stats2", "mean2", "norm2_ready", "s_done"))
        y_step, y_done, y_stored = sem("y_step"), sem("y_done"), sem("y_stored")

        A_UNITS = 4
        A_XT, A_GELU, A_Z, A_ZG = range(A_UNITS)
        M_UNITS = 12
        (U_QW, U_KW, U_VW, U_COMP, U_SEL, U_SELT, U_QK, U_V,
         U_VWW, U_VWC, U_PTW, U_PTC) = range(M_UNITS)

        def a_unit(b, k):
            return A_UNITS * b + k

        def m_unit(b, k):
            return A_UNITS * B + M_UNITS * b + k

        x_v = x.rearrange("b (t p) d -> p (b t) d", p=P)
        out_v = out.rearrange("b (t p) d -> p (b t) d", p=P)

        CONSTS = 4 + WPT

        passed = {e: sem(f"passed_{i}") for i, e in enumerate(nc.engines)}

        def wait_reg(eng, signal, value):
            eng.wait_ge(signal, value)
            if not isinstance(value, int):
                eng.sem_inc(passed[eng.engine], 1)

        block = ctx.enter_context(nc.Block())

        @block.sync
        def _(sp):
            sp.dma_start(x_sb[:, 0:2 * TB, :], x_v[:, 0:2 * TB, :]).then_inc(x_first, 16)
            sp.dma_start(x_sb[:, 2 * TB:, :], x_v[:, 2 * TB:, :]).then_inc(x_rest, 16)
            sp.dma_start(wo_sb[:, :, :], wo.rearrange("(r p) n -> p r n", p=P)).then_inc(w_late, 16)
            sp.dma_start(wc_sb[:, :, :], wc.rearrange("(r p) n -> p r n", p=P)).then_inc(w_late, 16)
            sp.dma_start(bo_row[:, :], bo.rearrange("(a n) -> a n", a=1)).then_inc(w_late, 16)

            def store_pair(p):
                for s in range(2):
                    b = 2 * p + s
                    sp.wait_ge(xn_done, b + 1)
                    sp.dma_start(xn_all[:, bass.ts(b, TB), :], xns[s][:, :, :]).then_inc(xn_stored[s], 16)
                    sp.wait_ge(unit_out, a_unit(b, A_Z) + 1)
                    sp.dma_start(zrow[:, bass.ts(b, L)], zs[s][0:1, :]).then_inc(z_stored[s], 16)

            def load_tiles(b, reload=True):
                for j in range(TB):
                    if reload:
                        sp.wait_ge(sim_ready, TB * (b - 1) + j + 1)
                    sp.dma_start(xTc[:, j, :], xT_all[:, bass.ds((TB * b + j) * P, P)]).then_inc(tile_in[j], 16)

            store_pair(0)
            load_tiles(0, reload=False)
            with sp.Fori(1, B // 2) as p:
                store_pair(p)
            for s in range(2):
                sp.wait_ge(z_stored[s], 16 * (B // 2))
            sp.dma_start(sc8[:, :], zrow[0:1, :].rearrange("a (b l) -> a b l", b=B)).then_inc(sc8_in, 16)

            def store_y(b):
                sp.wait_ge(y_done, b + 1)
                sp.dma_start(out_v[:, bass.ts(b, TB), :], y_sb[:, :, :]).then_inc(y_stored, 16)

            sp.wait_ge(rank_out, 1)
            sp.dma_start(rank32[:, :], sel_rank[:, :].rearrange("b (t l) -> b t l", t=TB)).then_inc(y_stored, 16)
            load_tiles(1)
            with sp.Fori(2, B) as b:
                load_tiles(b)
                store_y(b - 2)
            store_y(B - 2)
            store_y(B - 1)
            sp.wait_ge(y_stored, 16 * (B + 1))

        @block.gpsimd
        def _(pool):
            for half in range(2):
                pool.dma_start(fwq_sb[half * DKEY:(half + 1) * DKEY, :, :],
                               ffn_wq[bass.ts(half, HEADS * DKEY), :].rearrange("(h c) d -> c h d", h=HEADS)
                               ).then_inc(w_ffn, 16)
            pool.dma_start(keys_sb[:, :, :], ffn_keys.rearrange("(t h) k s c -> (h k) t (s c)", t=2)).then_inc(w_ffn, 16)
            for dst, src in ((down_sb, ffn_down), (up_sb, ffn_up)):
                for i0, rows, length, at in RUNS:
                    part = src[i0 * TOPK:(i0 + rows) * TOPK, :].rearrange("(i j) d -> i j d", j=TOPK)[:, 0:length, :]
                    pool.dma_start(dst[at:at + rows * length, :], part).then_inc(w_ffn, 16)
            steps = [0]

            def step(ins):
                steps[0] += 1
                ins.then_inc(consts, 1)
                pool.wait_ge(consts, steps[0])

            step(nc.gpsimd.memset(ident[:, :], 0.0))
            step(nc.gpsimd.affine_select(out=ident[:, :], in_=ident[:, :], compare_op=ALU.not_equal, fill=1.0,
                                         base=0, pattern=[[-1, P]], channel_multiplier=1))
            nc.gpsimd.memset(neg_half[:, :], -0.5)
            nc.gpsimd.memset(ones_row[:, :], 1.0)
            nc.gpsimd.memset(zero_row[:, :], 0.0)
            nc.gpsimd.memset(rsum[:, :], 1.0)
            nc.gpsimd.memset(pT_cs[:, :, :], 0.0)
            step(nc.gpsimd.memset(win_mask[:, :], TAKEN))
            for w in range(WPT):
                step(nc.gpsimd.memset(win_mask[w * WINDOW:(w + 1) * WINDOW, w * STEP_W:w * STEP_W + WINDOW], 0.0))
            step(nc.gpsimd.iota(rank_row[:, :], pattern=[[1, SELECT_K]], base=1, channel_multiplier=0,
                                allow_small_or_imprecise_dtypes=True))

            def rstd_pair(p):
                for s in range(2):
                    b = 2 * p + s
                    wait_reg(pool, mean1, b + 1)
                    nc.gpsimd.tensor_scalar(rstd1[s][:, :], mv1[s][:, :, 1], 1e-5, None, ALU.add).then_inc(pool_step, 1)
                    pool.wait_ge(pool_step, b + 1)
                    nc.gpsimd.tensor_tensor(rstd1[s][:, :], rstd1[s][:, :], neg_half[:, :],
                                            ALU.pow).then_inc(rstd1_done, 1)

            rstd_pair(0)
            with pool.Fori(1, B // 2) as p:
                rstd_pair(p)

            def build_cands(n, j, first):
                d = j % 2
                pool.wait_ge(top_done, 2 * n + 2)
                if not (first and n < 1):
                    pool.wait_ge(cand_ready, n)
                nc.gpsimd.tensor_tensor(shifted[:, :, :], top[d][:, :, :],
                                        top[d][:, :, 0:1].to_broadcast([P, VECS, TOPK]),
                                        ALU.subtract).then_inc(shift_done, 1)
                pool.wait_ge(shift_done, n + 1)
                if not (first and n < 2):
                    pool.wait_ge(left_done, 2 * n - 2)
                    pool.wait_ge(exp_done, n - 1)
                for i0, rows, length, at in RUNS:
                    o = cand[d][:, :, at:at + rows * length].rearrange("p h (i j) -> p h i j", i=rows)
                    a = shifted[:, 0:HEADS, i0:i0 + rows].unsqueeze(3).to_broadcast([P, HEADS, rows, length])
                    c = shifted[:, HEADS:VECS, 0:length].unsqueeze(2).to_broadcast([P, HEADS, rows, length])
                    last = nc.gpsimd.tensor_tensor(o, a, c, ALU.add)
                last.then_inc(cand_ready, 1)

            def weigh(n, j, first=False):
                d = j % 2
                pool.wait_ge(exp_done, n + 1)
                if not (first and n < 1):
                    pool.wait_ge(wgt_done, n)
                nc.gpsimd.tensor_tensor(prob[:, :, :], e_all[d][:, :, :], e_left[d][:, :, :],
                                        ALU.subtract).then_inc(prob_done, 1)
                pool.wait_ge(prob_done, n + 1)
                pool.wait_ge(rden_done, n + 1)
                if not (first and n < 2):
                    pool.wait_ge(c_ready, n - 1)
                nc.gpsimd.tensor_tensor(wgt[d][:, :, :], prob[:, :, :],
                                        rden[d][:, :].unsqueeze(2).to_broadcast([P, HEADS, CANDS]),
                                        ALU.mult).then_inc(wgt_done, 1)

            def gelu_times_weights(b):
                pool.wait_ge(c_out, b + 1)
                nc.gpsimd.tensor_tensor(actT[:, :], geluT[:, bass.ts(b, L)], c_sb[:, :],
                                        ALU.mult).then_inc(act_done, 1)

            def scale_probs(b):
                pool.wait_ge(rinv_done, b + 1)
                nc.gpsimd.tensor_tensor(rgate[:, 0:TB], rinv[:, 0:TB], gates[:, bass.ts(b, TB), WIN], ALU.mult)
                nc.gpsimd.tensor_tensor(rgate[:, TB:TB + 2], rinv[:, TB:TB + 2],
                                        gates[:, bass.ds(b * TB, 1), COMP:SEL + 1].rearrange("p a g -> p (a g)"),
                                        ALU.mult).then_inc(rgate_done, 1)
                pool.wait_ge(rgate_done, b + 1)
                nc.gpsimd.tensor_tensor(p_win[:, :, :], p_win[:, :, :],
                                        rgate[:, 0:TB].unsqueeze(2).to_broadcast([P, TB, WKEYS]), ALU.mult)
                nc.gpsimd.tensor_tensor(p_cs[:, 0:BLOCKS], p_cs[:, 0:BLOCKS],
                                        rgate[:, TB:TB + 1].to_broadcast([P, BLOCKS]), ALU.mult)
                nc.gpsimd.tensor_tensor(p_cs[0:SELECT_K, BLOCKS:CS], p_cs[0:SELECT_K, BLOCKS:CS],
                                        rgate[0:SELECT_K, TB + 1:TB + 2].to_broadcast([SELECT_K, SELECT_K]),
                                        ALU.mult).then_inc(p_scaled, 1)

            def norm2(b):
                wait_reg(pool, mean2, b + 1)
                nc.gpsimd.tensor_scalar(var2[:, :], mv2[:, :, 1], 4e-6, None, ALU.add).then_inc(pool_step, 1)
                pool.wait_ge(pool_step, B + 3 * b + 1)
                nc.gpsimd.tensor_tensor(rstd2[:, :], var2[:, :], neg_half[:, :], ALU.pow).then_inc(pool_step, 1)
                pool.wait_ge(pool_step, B + 3 * b + 2)
                nc.gpsimd.tensor_tensor(prod2[:, :], mv2[:, :, 0], rstd2[:, :], ALU.mult).then_inc(pool_step, 1)
                wait_reg(pool, pool_step, B + 3 * b + 3)
                nc.gpsimd.tensor_scalar(nmr2[:, :], prod2[:, :], -1.0, None, ALU.mult).then_inc(norm2_ready, 1)

            def finish_rows(b):
                pool.wait_ge(f_out, b + 1)
                nc.gpsimd.tensor_tensor(y1[:, :, :], half_f[:, :, :], tanh_f[:, :, :], ALU.mult).then_inc(y_step, 1)
                pool.wait_ge(y_step, 3 * b + 1)
                nc.gpsimd.tensor_tensor(y2[:, :, :], y1[:, :, :], half_f[:, :, :], ALU.add).then_inc(y_step, 1)
                pool.wait_ge(y_step, 3 * b + 2)
                pool.wait_ge(s_done, b + 1)
                nc.gpsimd.tensor_tensor(y3[:, :, :], y2[:, :, :], s_norm[:, :, :], ALU.mult).then_inc(y_step, 1)
                pool.wait_ge(y_step, 3 * b + 3)
                pool.wait_ge(y_stored, 16 * (b + 1))
                nc.gpsimd.tensor_tensor(y_sb[:, :, :], y3[:, :, :], x_sb[:, bass.ts(b, TB), :],
                                        ALU.add).then_inc(y_done, 1)

            def body(b, first=False):
                for j in range(TB):
                    n = TB * b + j
                    if j == TB - 1:
                        scale_probs(b)
                    if not (first and n < 2):
                        weigh(n - 2, j, first)
                    if j == 2 and not first:
                        gelu_times_weights(b - 1)
                    build_cands(n, j, first)
                    if j == 0 and not first:
                        norm2(b - 1)
                    if j == TB - 1 and not first:
                        finish_rows(b - 1)

            body(0, first=True)
            with pool.Fori(1, B) as b:
                body(b)
            weigh(TILES - 2, 0)
            norm2(B - 1)
            weigh(TILES - 1, 1)
            gelu_times_weights(B - 1)
            finish_rows(B - 1)

        @block.scalar
        def _(act):
            for dst, src in ((wq_sb, wq), (wk_sb, wk), (wv_sb, wv)):
                act.dma_start(dst[:, :], src[:, :]).then_inc(w_att, 16)
            act.dma_start(wz_sb[:, 0:1], ws[:, :]).then_inc(w_att, 16)
            act.dma_start(wz_sb[:, 1:4], wg[:, :]).then_inc(w_att, 16)
            for dst, src in ((bq_sb, bq), (bk_sb, bk), (bv_sb, bv), (bc_sb, bc)):
                act.dma_start(dst[:, :], src.rearrange("(n a) -> n a", a=1)).then_inc(w_att, 16)
            act.dma_start(bz_sb[0:1, :], bs.rearrange("(n a) -> n a", a=1)).then_inc(w_att, 16)
            act.dma_start(bz_sb[1:4, :], bg.rearrange("(n a) -> n a", a=1)).then_inc(w_att, 16)
            act.wait_ge(w_att, 16 * 11)
            nc.scalar.activation(bqs_sb[:, :], bq_sb[:, :], ACT.Copy, scale=SCALE)

            def prologue_pair(p, first=False):
                for s in range(2):
                    b = 2 * p + s
                    act.wait_ge(unit_full, a_unit(b, A_XT) + 1)
                    nc.scalar.activation(xT_all[:, bass.ts(b, L)], scratch[A_XT % 2][:, :],
                                         ACT.Copy).then_inc(unit_out, 1)
                    act.wait_ge(unit_full, a_unit(b, A_GELU) + 1)
                    nc.scalar.activation(geluT[:, bass.ts(b, L)], scratch[A_GELU % 2][0:CANDS, :],
                                         ACT.Gelu).then_inc(unit_out, 1)
                    act.wait_ge(unit_full, a_unit(b, A_Z) + 1)
                    if not first:
                        act.wait_ge(z_stored[s], 16 * p)
                        act.wait_ge(unit_full, a_unit(b - 2, A_ZG) + 1)
                    nc.scalar.activation(zs[s][:, :], scratch[A_Z % 2][0:4, :], ACT.Identity,
                                         bias=bz_sb[:, 0:1]).then_inc(unit_out, 1)
                    act.wait_ge(unit_full, a_unit(b, A_ZG) + 1)
                    nc.scalar.activation(zg[:, bass.ts(b, TB), :],
                                         scratch[A_ZG % 2][:, 0:4 * TB].rearrange("p (t g) -> p t g", t=TB),
                                         ACT.Copy).then_inc(unit_out, 1)

            prologue_pair(0, first=True)
            with act.Fori(1, B // 2) as p:
                prologue_pair(p)
            act.wait_ge(unit_out, A_UNITS * B)
            nc.scalar.activation(gexp[:, :, :], zg[:, :, 1:4], ACT.Exp, scale=-1.0).then_inc(gate_exp, 1)

            def exps(n, j, first=False):
                d = j % 2
                act.wait_ge(best_done, 2 * n + 2)
                if not (first and n < 2):
                    act.wait_ge(rden_done, n - 1)
                nc.scalar.activation(e_best[d][:, :, :], best[d][:, :, :], ACT.Exp).then_inc(exp_best, 1)
                if not (first and n < 2):
                    act.wait_ge(wgt_done, n - 1)
                nc.scalar.activation(e_all[d][:, :, :], cand[d][:, :, :], ACT.Exp)
                act.wait_ge(left_done, 2 * n + 2)
                nc.scalar.activation(e_left[d][:, :, :], left[d][:, :, :], ACT.Exp).then_inc(exp_done, 1)

            def unit(b, k, outs):
                act.wait_ge(unit_full, m_unit(b, k) + 1)
                for dst, cols, bias, scale in outs:
                    src = scratch[k % 2][0:dst.shape[0], cols:cols + dst.shape[1]]
                    if bias is None:
                        last = nc.scalar.activation(dst, src, ACT.Copy)
                    else:
                        last = nc.scalar.activation(dst, src, ACT.Identity, bias=bias[:, 0:1], scale=scale)
                last.then_inc(unit_out, 1)

            def norm_attention(b):
                act.wait_ge(norm2_ready, b + 1)
                for j in range(TB):
                    last = nc.scalar.activation(s_norm[:, j, :], out_bank[:, bass.ts(j, D)], ACT.Identity,
                                                bias=nmr2[:, j:j + 1], scale=rstd2[:, j:j + 1])
                last.then_inc(s_done, 1)

            def weights_out(b):
                act.wait_ge(c_ready, TB * b + TB)
                nc.scalar.activation(c_sb[:, :], c_bank[0:CANDS, :], ACT.Copy).then_inc(c_out, 1)

            def silu_parts(b):
                act.wait_ge(f_ready, b + 1)
                f_v = f_bank[:, :].rearrange("p (t d) -> p t d", t=TB)
                nc.scalar.activation(tanh_f[:, :, :], f_v, ACT.Tanh, scale=0.5)
                nc.scalar.activation(half_f[:, :, :], f_v, ACT.Copy, scale=0.5).then_inc(f_out, 1)

            def body(b, first=False):
                for j in range(TB):
                    n = TB * b + j
                    if not (first and n < 2):
                        exps(n - 2, j, first)
                    if j == 0:
                        act.wait_ge(unit_full, m_unit(b, U_QW) + 1)
                        overlap = bass.AP(scratch[U_QW % 2], 0, [[512, P], [STEP_W, L // WINDOW], [1, WINDOW]])
                        nc.scalar.activation(qw[:, :].rearrange("p (w t) -> p w t", t=WINDOW), overlap, ACT.Identity,
                                             bias=bqs_sb[:, 0:1], scale=SCALE).then_inc(unit_out, 1)
                        unit(b, U_KW, [(kw[:, :], 0, bk_sb, 1.0)])
                        unit(b, U_VW, [(vw[:, :], 0, bv_sb, 1.0)])
                        unit(b, U_COMP, [(csT[:, 0:BLOCKS], 0, bc_sb, 1.0)])
                    if j == 1:
                        if not first:
                            norm_attention(b - 1)
                        unit(b, U_SEL, [(xsel[:, :], 0, None, 1.0)])
                        unit(b, U_SELT, [(csT[:, BLOCKS:CS], 0, None, 1.0)])
                        unit(b, U_QK, [(qcs[:, :], 0, bqs_sb, SCALE), (kcs[:, :], CS, bk_sb, 1.0)])
                        unit(b, U_V, [(vcs[:, :], 0, bv_sb, 1.0)])
                    if j == 2:
                        if not first:
                            weights_out(b - 1)
                        unit(b, U_VWW, [(vww[:, :, :].rearrange("p t d -> p (t d)"), 0, None, 1.0)])
                        unit(b, U_VWC, [(vwc[:, :, :].rearrange("p t d -> p (t d)"), 0, None, 1.0)])
                        act.wait_ge(max_done, b + 1)
                        for g in range(TB):
                            nc.scalar.activation(p_win[:, g, :], s_win[:, g, :], ACT.Exp,
                                                 bias=nmax[:, g:g + 1], accum_out=rsum[:, g:g + 1])
                        nc.scalar.activation(p_cs[:, 0:BLOCKS], s_bank[:, TB * WKEYS:TB * WKEYS + BLOCKS], ACT.Exp,
                                             bias=nmax[:, TB:TB + 1], accum_out=rsum[:, TB:TB + 1])
                        nc.scalar.activation(p_cs[0:SELECT_K, BLOCKS:CS],
                                             s_bank[0:SELECT_K, TB * WKEYS + BLOCKS:TB * WKEYS + CS], ACT.Exp,
                                             bias=nmax[0:SELECT_K, TB + 1:TB + 2],
                                             accum_out=rsum[0:SELECT_K, TB + 1:TB + 2]).then_inc(p_exp, 1)
                    if j == 3:
                        if not first:
                            silu_parts(b - 1)
                        unit(b, U_PTW, [(pT_win[:, :, :].rearrange("p t q -> p (t q)"), 0, None, 1.0)])
                        unit(b, U_PTC, [(pT_cs[:, 0, :], 0, None, 1.0),
                                        (pT_cs[0:SELECT_K, 1, 0:SELECT_K], P, None, 1.0)])

            body(0, first=True)
            with act.Fori(1, B) as b:
                body(b)
            exps(TILES - 2, 0)
            norm_attention(B - 1)
            exps(TILES - 1, 1)
            weights_out(B - 1)
            silu_parts(B - 1)

        @block.vector
        def _(dve):
            dve.wait_ge(prep_pe, 1)
            nc.vector.tensor_copy(keysT[:, :], f_bank[:, 0:HK])
            nc.vector.tensor_copy(downT[:, :], c_bank[:, 0:CANDS]).then_inc(prep_dve, 1)

            def stats_of(src, st, mv, counter, before, done):
                for j in range(TB):
                    last = nc.vector.bn_stats(st[:, j, :], src(j))
                last.then_inc(counter, 1)
                wait_reg(dve, counter, before + 1)
                for j in range(TB):
                    last = nc.vector.bn_aggr(mv[:, j, :], st[:, j, :])
                last.then_inc(done, 1)

            def prologue_pair(p, first=False):
                for s in range(2):
                    b = 2 * p + s
                    if not first:
                        dve.wait_ge(xn_done, 2 * p)
                        wait_reg(dve, mean1, b)
                    elif s == 1:
                        dve.wait_ge(mean1, 1)
                    stats_of(lambda j: x_sb[:, bass.ds(TB * b + j, 1), :].rearrange("p a d -> p (a d)"),
                             st1, mv1[s], stats1, b, mean1)
                for s in range(2):
                    b = 2 * p + s
                    dve.wait_ge(rstd1_done, b + 1)
                    if not first:
                        dve.wait_ge(unit_full, a_unit(b - 2, A_XT) + 1)
                        dve.wait_ge(xn_stored[s], 16 * p)
                    for j in range(TB):
                        last = nc.vector.tensor_scalar(
                            xns[s][:, j, :], x_sb[:, bass.ds(TB * b + j, 1), :].rearrange("p a d -> p (a d)"),
                            mv1[s][:, j, 0:1], rstd1[s][:, j:j + 1], ALU.subtract, ALU.mult)
                    last.then_inc(xn_done, 1)

            dve.wait_ge(x_first, 16)
            prologue_pair(0, first=True)
            dve.wait_ge(prep_pe, 2)
            nc.vector.tensor_copy(sim_w[:, 0:HK], s_bank[:, 0:HK])
            nc.vector.tensor_copy(sim_w[:, HK:2 * HK], out_bank[:, 0:HK]).then_inc(prep_dve, 1)
            dve.wait_ge(x_rest, 16)
            with dve.Fori(1, B // 2) as p:
                prologue_pair(p)

            def denominators(n, j, first):
                d = j % 2
                if not (first and n < 1):
                    dve.wait_ge(rden_done, n)
                dve.wait_ge(exp_best, n + 1)
                nc.vector.tensor_reduce(den[:, :], e_best[d][:, :, :], AX_X, ALU.add).then_inc(den_done, 1)
                dve.wait_ge(den_done, n + 1)
                if not (first and n < 2):
                    dve.wait_ge(wgt_done, n - 1)
                nc.vector.reciprocal(rden[d][:, :], den[:, :]).then_inc(rden_done, 1)

            def sort_scores(n, j, first=False, tail=None):
                d = j % 2
                if not (first and n < 2):
                    dve.wait_ge(shift_done, n - 1)
                wait_reg(dve, sim_ready, n + 1)
                for h in range(2):
                    for v in range(h * HALF_V, (h + 1) * HALF_V):
                        last = nc.vector.max(top[d][:, v, 0:8], sim_bank[d][:, bass.ts(v, KEYS)])
                    last.then_inc(sim_top8, 1)
                if tail is not None:
                    tail()
                for h in range(2):
                    if not (first and n < 1):
                        dve.wait_ge(top_done, 2 * n - 1 + h)
                    wait_reg(dve, sim_top8, 2 * n + 1 + h)
                    for v in range(h * HALF_V, (h + 1) * HALF_V):
                        last = nc.vector.match_replace(out=rest[:, v, :], in_to_replace=top[d][:, v, 0:8],
                                                       in_values=sim_bank[d][:, bass.ts(v, KEYS)],
                                                       imm_value=NO_SCORE)
                    last.then_inc(sim_used, 1)
                for h in range(2):
                    wait_reg(dve, sim_used, 2 * n + 1 + h)
                    for v in range(h * HALF_V, (h + 1) * HALF_V):
                        last = nc.vector.max(top[d][:, v, 8:16], rest[:, v, :])
                    last.then_inc(top_done, 1)

            def take_best(n, j, first=False):
                d = j % 2
                halves = [range(h * HALF_H, (h + 1) * HALF_H) for h in range(2)]
                if not (first and n < 2):
                    dve.wait_ge(exp_best, n - 1)
                wait_reg(dve, cand_ready, n + 1)
                for hs in halves:
                    for h in hs:
                        last = nc.vector.max(best[d][:, h, 0:8], cand[d][:, h, :])
                    last.then_inc(best8, 1)
                if not (first and n < 1):
                    dve.wait_ge(left_done, 2 * n)
                for k, hs in enumerate(halves):
                    wait_reg(dve, best8, 2 * n + 1 + k)
                    for h in hs:
                        last = nc.vector.match_replace(out=crest[:, h, :], in_to_replace=best[d][:, h, 0:8],
                                                       in_values=cand[d][:, h, :], imm_value=TAKEN)
                    last.then_inc(best8_out, 1)
                for k, hs in enumerate(halves):
                    wait_reg(dve, best8_out, 2 * n + 1 + k)
                    for h in hs:
                        last = nc.vector.max(best[d][:, h, 8:16], crest[:, h, :])
                    last.then_inc(best_done, 1)
                if not (first and n < 2):
                    dve.wait_ge(exp_done, n - 1)
                for k, hs in enumerate(halves):
                    wait_reg(dve, best_done, 2 * n + 1 + k)
                    for h in hs:
                        last = nc.vector.match_replace(out=left[d][:, h, :], in_to_replace=best[d][:, h, 8:16],
                                                       in_values=crest[:, h, :], imm_value=TAKEN)
                    last.then_inc(left_done, 1)

            def chain(n_done, ins):
                ins.then_inc(sel_step, 1)
                dve.wait_ge(sel_step, n_done)

            def select_tokens():
                dve.wait_ge(sc8_in, 16)
                k = 0
                src, dst = sc8, sel_a
                for r in range(SELECT_K // 8):
                    k += 1
                    chain(k, nc.vector.max(sel_m[:, :], src[:, :]))
                    k += 1
                    chain(k, nc.vector.match_replace(out=dst[:, :], in_to_replace=sel_m[:, :],
                                                     in_values=src[:, :], imm_value=NO_SCORE))
                    src, dst = dst, (sel_b if dst is sel_a else sel_a)
                k += 1
                chain(k, nc.vector.tensor_scalar(sel_mask[:, :], src[:, :], NO_SCORE, None, ALU.is_equal))
                k += 1
                chain(k, nc.vector.tensor_tensor_scan(sel_cnt[:, :], sel_mask[:, :], zero_row[0:B, :], 0.0,
                                                      ALU.add, ALU.add))
                nc.vector.tensor_tensor(sel_rank[:, :], sel_cnt[:, :], sel_mask[:, :], ALU.mult).then_inc(rank_out, 1)

            def normalise_gates():
                dve.wait_ge(gate_exp, 1)
                k = [0]

                def link(ins):
                    k[0] += 1
                    ins.then_inc(gate_step, 1)
                    dve.wait_ge(gate_step, k[0])

                link(nc.vector.tensor_scalar(gexp[:, :, :], gexp[:, :, :], 1.0, None, ALU.add))
                link(nc.vector.reciprocal(gsig[:, :, :], gexp[:, :, :]))
                link(nc.vector.tensor_reduce(gsum[:, :], gsig[:, :, :], AX_X, ALU.add))
                link(nc.vector.tensor_scalar(gsum[:, :], gsum[:, :], 1e-6, None, ALU.add))
                link(nc.vector.reciprocal(gsum[:, :], gsum[:, :]))
                link(nc.vector.tensor_tensor(gates[:, :, :], gsig[:, :, :],
                                             gsum[:, :].unsqueeze(2).to_broadcast([P, TILES, 3]), ALU.mult))

            def pick_matrix(b):
                for j in range(TB):
                    last = nc.vector.tensor_scalar(pick[:, j, :], rank_row[:, :],
                                                   rankT[:, bass.ds(TB * b + j, 1)], None, ALU.is_equal)
                last.then_inc(pick_done, 1)

            def maxima(b):
                dve.wait_ge(s_ready, b + 1)
                nc.vector.tensor_tensor(s_win[:, :, :], s_bank[:, 0:TB * WKEYS].rearrange("p (g k) -> p g k", g=TB),
                                        win_mask[:, :].unsqueeze(1).to_broadcast([P, TB, WKEYS]),
                                        ALU.add).then_inc(s_masked, 1)
                nc.vector.tensor_reduce(nmax[:, TB:TB + 1], s_bank[:, TB * WKEYS:TB * WKEYS + BLOCKS], AX_X, ALU.max,
                                        negate=True)
                nc.vector.tensor_reduce(nmax[0:SELECT_K, TB + 1:TB + 2],
                                        s_bank[0:SELECT_K, TB * WKEYS + BLOCKS:TB * WKEYS + CS], AX_X, ALU.max,
                                        negate=True)
                dve.wait_ge(s_masked, b + 1)
                nc.vector.tensor_reduce(nmax[:, 0:TB], s_win[:, :, :], AX_X, ALU.max, negate=True).then_inc(max_done, 1)

            def norm2_stats(b):
                dve.wait_ge(out_ready, b + 1)
                stats_of(lambda j: out_bank[:, bass.ts(j, D)], st2, mv2, stats2, b, mean2)

            def body(b, first=False):
                for j in range(TB):
                    n = TB * b + j
                    tail = (lambda: denominators(n - 2, j, first)) if not (first and n < 2) else None
                    sort_scores(n, j, first, tail)
                    if first and j == 0:
                        dve.wait_ge(consts, CONSTS)
                        select_tokens()
                    if j == 0 and not first:
                        norm2_stats(b - 1)
                    if j == 2:
                        maxima(b)
                    if not (first and n < 1):
                        take_best(n - 1, j - 1, first)
                    if first and j == 1:
                        normalise_gates()
                        dve.wait_ge(rankT_ready, 1)
                        nc.vector.tensor_copy(rankT[:, :], f_bank[:, 0:TILES]).then_inc(rankT_out, 1)
                        dve.wait_ge(rankT_out, 1)
                        pick_matrix(0)
                    if j == 0 and not first:
                        pick_matrix(b)
                    if j == 2:
                        dve.wait_ge(p_exp, b + 1)
                        nc.vector.reciprocal(rinv[:, :], rsum[:, :]).then_inc(rinv_done, 1)

            body(0, first=True)
            with dve.Fori(1, B) as b:
                body(b)
            denominators(TILES - 2, 0, False)
            norm2_stats(B - 1)
            take_best(TILES - 1, 1)
            denominators(TILES - 1, 1, False)

        @block.tensor
        def _(pe):
            mm = nc.tensor.matmul

            pe.wait_ge(consts, CONSTS)
            pe.wait_ge(w_ffn, 16 * (3 + 2 * len(RUNS)))
            for t in range(2):
                nc.tensor.transpose(f_bank[:, bass.ts(t, P)], keys_sb[:, t, :], ident[:, :])
            nc.tensor.transpose(c_bank[:, 0:CANDS], down_sb[:, :], ident[0:CANDS, 0:CANDS]).then_inc(prep_pe, 1)
            pe.wait_ge(prep_dve, 1)
            for half, dst in enumerate((s_bank, out_bank)):
                for h in range(HEADS):
                    last = mm(dst[:, bass.ts(h, KEYS)], fwq_sb[half * DKEY:(half + 1) * DKEY, h, :],
                              keysT[half * DKEY:(half + 1) * DKEY, bass.ts(h, KEYS)], start=True, stop=True)
            last.then_inc(prep_pe, 1)

            def fill(u, parity, after=None):
                wait_reg(pe, unit_out, u - 1)
                if after is not None:
                    wait_reg(pe, unit_out, after + 1)
                return scratch[parity]

            def prologue_pair(p, first=False):
                for s in range(2):
                    b = 2 * p + s
                    rows = xT_all[:, bass.ts(b, L)]
                    if not (first and s == 0):
                        pe.wait_ge(unit_out, a_unit(b, A_XT) - 1)
                    pe.wait_ge(xn_done, b + 1)
                    for j in range(TB):
                        last = nc.tensor.transpose(scratch[0][:, bass.ts(j, P)], xns[s][:, j, :], ident[:, :])
                    last.then_inc(unit_full, 1)
                    pe.wait_ge(unit_out, a_unit(b, A_XT) + 1)
                    mm(scratch[1][0:CANDS, :], downT[:, :], rows, start=True, stop=True).then_inc(unit_full, 1)
                    mm(scratch[0][0:4, :], wz_sb[:, :], rows, start=True, stop=True).then_inc(unit_full, 1)
                    wait_reg(pe, unit_out, a_unit(b, A_Z) + 1)
                    for j in range(TB):
                        last = nc.tensor.transpose(scratch[1][:, bass.ts(j, 4)], zs[s][:, bass.ts(j, P)],
                                                   ident[0:4, 0:4])
                    last.then_inc(unit_full, 1)

            def scores(n, j, b, first=False):
                pe.wait_ge(tile_in[j], 16 * (b + 1))
                if not (first and n < 2):
                    pe.wait_ge(sim_used, 2 * n - 2)
                mm(sim_bank[j % 2][:, :], xTc[:, j, :], sim_w[:, :], start=True, stop=True).then_inc(sim_ready, 1)

            def expert_weights(n, j, first=False):
                d = j % 2
                pe.wait_ge(wgt_done, n + 1)
                for h in range(HEADS):
                    last = mm(c_bank[0:CANDS, bass.ts(j, P)], wgt[d][:, h, :], ident[:, :],
                              start=(h == 0), stop=(h == HEADS - 1))
                last.then_inc(c_ready, 1)

            def experts_out(b):
                pe.wait_ge(act_done, b + 1)
                for j in range(TB):
                    last = mm(f_bank[:, bass.ts(j, D)], actT[:, bass.ts(j, P)], up_sb[:, :], start=True, stop=True)
                last.then_inc(f_ready, 1)

            def project_windows(b):
                for k, w in ((U_QW, wq_sb), (U_KW, wk_sb), (U_VW, wv_sb)):
                    o = fill(m_unit(b, k), k % 2)
                    mm(o[:, 0:WTOK], w[:, :], xT_all[:, bass.ds(b * L, WTOK)],
                       start=True, stop=True).then_inc(unit_full, 1)
                o = fill(m_unit(b, U_COMP), U_COMP % 2)
                rows = xT_all[:, bass.ts(b, L)].rearrange("p (c r) -> p r c", r=RATIO)
                for r in range(RATIO):
                    last = mm(o[:, 0:BLOCKS], wc_sb[:, r, :], rows[:, r, :], start=(r == 0), stop=(r == RATIO - 1))
                last.then_inc(unit_full, 1)

            def project_selected(b):
                pe.wait_ge(pick_done, b + 1)
                o = fill(m_unit(b, U_SEL), U_SEL % 2)
                for j in range(TB):
                    last = mm(o[0:SELECT_K, 0:D], pick[:, j, :],
                              xn_all[:, bass.ds(b * TB + j, 1), :].rearrange("p a d -> p (a d)"),
                              start=(j == 0), stop=(j == TB - 1))
                last.then_inc(unit_full, 1)
                o = fill(m_unit(b, U_SELT), U_SELT % 2, m_unit(b, U_SEL))
                nc.tensor.transpose(o[:, 0:SELECT_K], xsel[:, :], ident[0:SELECT_K, 0:SELECT_K]).then_inc(unit_full, 1)
                o = fill(m_unit(b, U_QK), U_QK % 2, m_unit(b, U_SELT))
                mm(o[:, 0:CS], wq_sb[:, :], csT[:, :], start=True, stop=True)
                mm(o[:, CS:2 * CS], wk_sb[:, :], csT[:, :], start=True, stop=True).then_inc(unit_full, 1)
                o = fill(m_unit(b, U_V), U_V % 2)
                mm(o[:, 0:CS], wv_sb[:, :], csT[:, :], start=True, stop=True).then_inc(unit_full, 1)

            def attention_scores(b, first=False):
                pe.wait_ge(unit_out, m_unit(b, U_QK) + 1)
                if not first:
                    pe.wait_ge(p_exp, b)
                for g in range(TB):
                    k0 = g * WPT * STEP_W
                    mm(s_bank[:, bass.ts(g, WKEYS)], qw[:, bass.ts(g, P)], kw[:, k0:k0 + WKEYS], start=True, stop=True)
                c0 = TB * WKEYS
                mm(s_bank[:, c0:c0 + BLOCKS], qcs[:, 0:BLOCKS], kcs[:, 0:BLOCKS], start=True, stop=True)
                mm(s_bank[0:SELECT_K, c0 + BLOCKS:c0 + CS], qcs[:, BLOCKS:CS], kcs[:, BLOCKS:CS],
                   start=True, stop=True).then_inc(s_ready, 1)

            def values_out(b):
                o = fill(m_unit(b, U_VWW), U_VWW % 2, m_unit(b, U_V))
                for g in range(TB):
                    k0 = g * WPT * STEP_W
                    last = mm(o[0:WKEYS, bass.ts(g, D)], vw[:, k0:k0 + WKEYS], wo_sb[:, WIN, :], start=True, stop=True)
                last.then_inc(unit_full, 1)
                o = fill(m_unit(b, U_VWC), U_VWC % 2)
                mm(o[:, 0:D], vcs[:, 0:BLOCKS], wo_sb[:, COMP, :], start=True, stop=True)
                mm(o[0:SELECT_K, D:2 * D], vcs[:, BLOCKS:CS], wo_sb[:, SEL, :], start=True, stop=True).then_inc(unit_full, 1)

            def attention_out(b, first=False):
                pe.wait_ge(p_scaled, b + 1)
                o = fill(m_unit(b, U_PTW), U_PTW % 2)
                for g in range(TB):
                    last = nc.tensor.transpose(o[0:WKEYS, bass.ts(g, P)], p_win[:, g, :], ident[:, :])
                last.then_inc(unit_full, 1)
                o = fill(m_unit(b, U_PTC), U_PTC % 2)
                nc.tensor.transpose(o[:, 0:P], p_cs[:, 0:BLOCKS], ident[:, :])
                nc.tensor.transpose(o[0:SELECT_K, P:P + SELECT_K], p_cs[0:SELECT_K, BLOCKS:CS],
                                    ident[0:SELECT_K, 0:SELECT_K]).then_inc(unit_full, 1)
                pe.wait_ge(unit_out, m_unit(b, U_PTC) + 1)
                if not first:
                    pe.wait_ge(s_done, b)
                for j in range(TB):
                    o = out_bank[:, bass.ts(j, D)]
                    mm(o, ident[:, :], xn_all[:, bass.ds(b * TB + j, 1), :].rearrange("p a d -> p (a d)"),
                       start=True, stop=False)
                    mm(o, ones_row[:, :], bo_row[:, :], start=False, stop=False)
                    if j == 0:
                        mm(o, pT_cs[:, 0, :], vwc[:, 0, :], start=False, stop=False)
                        mm(o, pT_cs[0:SELECT_K, 1, :], vwc[0:SELECT_K, 1, :], start=False, stop=False)
                    last = mm(o, pT_win[:, j, :], vww[:, j, :], start=False, stop=True)
                last.then_inc(out_ready, 1)

            def body(b, first=False):
                for j in range(TB):
                    n = TB * b + j
                    scores(n, j, b, first)
                    if j == 0:
                        project_windows(b)
                    if j == 1:
                        if first:
                            pe.wait_ge(y_stored, 16)
                            nc.tensor.transpose(f_bank[:, 0:TILES], rank32[:, :],
                                                ident[0:TILES, 0:TILES]).then_inc(rankT_ready, 1)
                        project_selected(b)
                        attention_scores(b, first)
                    if j == 2:
                        values_out(b)
                        if not first:
                            experts_out(b - 1)
                    if j == 3:
                        attention_out(b, first)
                    if not (first and n < 2):
                        if j == 2:
                            pe.wait_ge(c_out, b)
                        expert_weights(n - 2, (j + 2) % TB, first)

            pe.wait_ge(w_att, 16 * 11)
            prologue_pair(0, first=True)
            with pe.Fori(1, B // 2) as p:
                prologue_pair(p)
            pe.wait_ge(w_late, 16 * 3)
            for s in range(2):
                pe.wait_ge(xn_stored[s], 16 * (B // 2))
            pe.wait_ge(prep_dve, 2)
            body(0, first=True)
            with pe.Fori(1, B) as b:
                body(b)
            expert_weights(TILES - 2, 2)
            expert_weights(TILES - 1, 3)
            experts_out(B - 1)


_INS = ["L0_attn_hidden_states", "L0_attn_Wq", "L0_attn_bq", "L0_attn_Wk", "L0_attn_bk", "L0_attn_Wv",
        "L0_attn_bv", "L0_attn_Wo", "L0_attn_bo", "L0_attn_Wg", "L0_attn_bg", "L0_attn_Wc", "L0_attn_bc",
        "L0_attn_Ws", "L0_attn_bs", "L0_ffn_Wq", "L0_ffn_keys", "L0_ffn_W_down", "L0_ffn_W_up"]


def kernel(**inputs):
    import numpy as np
    import concourse.bacc as bacc
    from concourse.bass_utils import run_bass_kernel_spmd

    nc = bacc.Bacc("TRN2", target_bir_lowering=False, num_devices=1)
    arrays, args = {}, []
    for name in _INS:
        a = np.ascontiguousarray(inputs[name])
        arrays[f"in_{name}"] = a
        args.append(nc.dram_tensor(f"in_{name}", a.shape, mybir.dt.from_np(a.dtype), kind="ExternalInput").ap())
    shape = inputs["L0_attn_hidden_states"].shape
    args.append(nc.dram_tensor("out_0", shape, F32, kind="ExternalOutput").ap())
    program(nc, *args)
    r = run_bass_kernel_spmd(nc, [arrays], core_ids=[0])
    return r.results[0]["out_0"]
```

```python
from contextlib import ExitStack

import concourse.bass as bass
from concourse import mybir
from concourse.alu_op_type import AluOpType as ALU

F32 = mybir.dt.float32
ACT = mybir.ActivationFunctionType
AX_X = mybir.AxisListType.X

P = 128
RATIO = 4
SELECT_K = 64
WINDOW = 32
STEP_W = WINDOW // 2
N_HEADS = 16
COMP, SEL, WIN = range(3)
HEADS = 8
KEYS = 32
DKEY = 64
TOPK = 16
VECS = 2 * HEADS
ROW_LEN = [TOPK // (i + 1) for i in range(TOPK)]
CANDS = sum(ROW_LEN)
RUNS = []
_at = 0
for _i, _n in enumerate(ROW_LEN):
    if RUNS and RUNS[-1][2] == _n:
        RUNS[-1][1] += 1
    else:
        RUNS.append([_i, 1, _n, _at])
    _at += _n
TAKEN = -1e30
NO_SCORE = -3.3e38
HALF_V = VECS // 2
HALF_H = HEADS // 2


def program(nc, x, wq, bq, wk, bk, wv, bv, wo, bo, wg, bg, wc, bc, ws, bs,
            ffn_wq, ffn_keys, ffn_down, ffn_up, out):
    B, L, D = x.shape
    assert D == P and L % P == 0 and B % 2 == 0
    TB = L // P
    TILES = B * TB
    BLOCKS = L // RATIO
    WPT = P // WINDOW
    WKEYS = STEP_W * (WPT - 1) + WINDOW
    WTOK = STEP_W * WPT * (TB - 1) + WKEYS
    CS = BLOCKS + SELECT_K
    SCALE = float((D // N_HEADS) ** -0.5)
    HK = HEADS * KEYS
    assert TB == 4 and BLOCKS == P and TB * WKEYS + CS <= 512 and 2 * HK <= 512

    ctx = ExitStack()
    with ctx:
        def sb(name, shape, dt=F32):
            return ctx.enter_context(nc.sbuf_tensor(name, shape, dt))

        def bank(name):
            return ctx.enter_context(nc.psum_tensor(name, [P, 512], F32))

        def sem(name):
            return ctx.enter_context(nc.semaphore(name))

        sim_bank = [bank(f"sim{i}") for i in range(2)]
        scratch = [bank(f"scratch{i}") for i in range(2)]
        s_bank = bank("s_bank")
        out_bank = bank("out_bank")
        c_bank = bank("c_bank")
        f_bank = bank("f_bank")
        h_bank = [c_bank, out_bank]

        ident = sb("ident", [P, P])
        ones_row = sb("ones_row", [1, P])
        rank_row = sb("rank_row", [P, SELECT_K])
        neg_half = sb("neg_half", [P, TB])
        win_mask = sb("win_mask", [P, WKEYS])
        wq_sb, wk_sb, wv_sb = (sb(n, [P, D]) for n in ("wq_sb", "wk_sb", "wv_sb"))
        wc_sb = sb("wc_sb", [P, RATIO, D])
        wo_sb = sb("wo_sb", [P, 3, D])
        wz_sb = sb("wz_sb", [P, 4])
        bq_sb, bqs_sb, bk_sb, bv_sb, bc_sb = (sb(n, [P, 1]) for n in ("bq_sb", "bqs_sb", "bk_sb", "bv_sb", "bc_sb"))
        bz_sb = sb("bz_sb", [4, 1])
        bo_row = sb("bo_row", [1, D])
        fwq_sb = sb("fwq_sb", [P, HEADS, D])
        keys_sb = sb("keys_sb", [P, 2, P])
        keysT = sb("keysT", [P, HK])
        sim_w = sb("sim_w", [P, VECS * KEYS])
        down_sb = sb("down_sb", [CANDS, D])
        downT = sb("downT", [P, CANDS])
        up_sb = sb("up_sb", [CANDS, D])

        x_sb = sb("x_sb", [P, TILES, D])
        xn_all = sb("xn_all", [P, TILES, D])
        xT_all = sb("xT_all", [P, TILES * P])
        xTc = sb("xTc", [P, TB, P])
        st1 = [sb(f"st1_{i}", [P, TB, 6]) for i in range(2)]
        mv1 = [sb(f"mv1_{i}", [P, TB, 2]) for i in range(2)]
        var1 = [sb(f"var1_{i}", [P, TB]) for i in range(2)]
        rstd1 = [sb(f"rstd1_{i}", [P, TB]) for i in range(2)]
        prod1 = [sb(f"prod1_{i}", [P, TB]) for i in range(2)]
        nmr1 = [sb(f"nmr1_{i}", [P, TB]) for i in range(2)]
        geluT = sb("geluT", [CANDS, TILES * P])
        zT_all = sb("zT_all", [4, TILES * P])
        gexp = sb("gexp", [P, TILES, 3])
        gsig = sb("gsig", [P, TILES, 3])
        gsum = sb("gsum", [P, TILES])
        gates = sb("gates", [P, TILES, 3])

        sc8 = sb("sc8", [B, L])
        sel_a = sb("sel_a", [B, L])
        sel_b = sb("sel_b", [B, L])
        sel_m = sb("sel_m", [B, 8])
        sel_mask = sb("sel_mask", [B, L])
        sel_cnt = sb("sel_cnt", [B, L])
        sel_rank = sb("sel_rank", [B, L])
        zero_row = sb("zero_row", [B, L])
        rank32 = sb("rank32", [TILES, P])
        rankT = sb("rankT", [P, TILES])
        pick = sb("pick", [P, TB, SELECT_K])

        qw = sb("qw", [P, L])
        kw, vw = (sb(n, [P, WTOK]) for n in ("kw", "vw"))
        xsel = sb("xsel", [SELECT_K, D])
        csT = sb("csT", [P, CS])
        qcs, kcs, vcs = (sb(n, [P, CS]) for n in ("qcs", "kcs", "vcs"))
        vww = sb("vww", [WKEYS, TB, D])
        vwc = sb("vwc", [P, 2, D])
        s_win = sb("s_win", [P, TB, WKEYS])
        nmax = sb("nmax", [P, 6])
        rsum = sb("rsum", [P, 6])
        rinv = sb("rinv", [P, 6])
        rgate = sb("rgate", [P, 6])
        p_win = sb("p_win", [P, TB, WKEYS])
        p_cs = sb("p_cs", [P, CS])
        pT_win = sb("pT_win", [WKEYS, TB, P])
        pT_cs = sb("pT_cs", [P, 2, P])
        st2 = sb("st2", [P, TB, 6])
        mv2 = sb("mv2", [P, TB, 2])
        var2 = sb("var2", [P, TB])
        rstd2 = sb("rstd2", [P, TB])
        prod2 = sb("prod2", [P, TB])
        nmr2 = sb("nmr2", [P, TB])
        s_norm = sb("s_norm", [P, TB, D])

        top = [sb(f"top{i}", [P, VECS, TOPK]) for i in range(2)]
        rest = sb("rest", [P, VECS, KEYS])
        shifted = sb("shifted", [P, VECS, TOPK])
        cand = [sb(f"cand{i}", [P, HEADS, CANDS]) for i in range(2)]
        crest = sb("crest", [P, HEADS, CANDS])
        left = [sb(f"left{i}", [P, HEADS, CANDS]) for i in range(2)]
        best = [sb(f"best{i}", [P, HEADS, TOPK]) for i in range(2)]
        e_best = [sb(f"e_best{i}", [P, HEADS, TOPK]) for i in range(2)]
        e_all = [sb(f"e_all{i}", [P, HEADS, CANDS]) for i in range(2)]
        e_left = [sb(f"e_left{i}", [P, HEADS, CANDS]) for i in range(2)]
        den = sb("den", [P, HEADS])
        rden = [sb(f"rden{i}", [P, HEADS]) for i in range(2)]
        prob = sb("prob", [P, HEADS, CANDS])
        wgt = [sb(f"wgt{i}", [P, HEADS, CANDS]) for i in range(2)]
        c_sb = sb("c_sb", [CANDS, L])
        actT = sb("actT", [CANDS, L])
        tanh_f = sb("tanh_f", [P, TB, D])
        half_f = sb("half_f", [P, TB, D])
        y1 = sb("y1", [P, TB, D])
        y2 = sb("y2", [P, TB, D])
        y3 = sb("y3", [P, TB, D])
        y_sb = sb("y_sb", [P, TB, D])

        x_in = [sem(f"x_in{i}") for i in range(3)]
        w_ffn, w_att, w_late = sem("w_ffn"), sem("w_att"), sem("w_late")
        W_FFN, W_ATT, W_LATE = 3 + len(RUNS), 4, 10 + len(RUNS)
        bqs_done = sem("bqs_done")
        consts = sem("consts")
        prep_pe, prep_dve = sem("prep_pe"), sem("prep_dve")
        stats1, mean1, norm1_ready, xn_done = sem("stats1"), sem("mean1"), sem("norm1_ready"), sem("xn_done")
        pool_step = sem("pool_step")
        xt_full, xt_out, h_full, gelu_done, z_full, z_out, zg_full, zg_out = (
            sem(n) for n in ("xt_full", "xt_out", "h_full", "gelu_done", "z_full", "z_out", "zg_full", "zg_out"))
        sc8_in = sem("sc8_in")
        unit_full, unit_out = sem("unit_full"), sem("unit_out")
        tile_in = [sem(f"tile_in{j}") for j in range(TB)]
        sim_ready, sim_top8, sim_used, top_done = sem("sim_ready"), sem("sim_top8"), sem("sim_used"), sem("top_done")
        shift_done, cand_ready = sem("shift_done"), sem("cand_ready")
        best8, best8_out, best_done, left_done = sem("best8"), sem("best8_out"), sem("best_done"), sem("left_done")
        exp_best, exp_done, den_done, rden_done = sem("exp_best"), sem("exp_done"), sem("den_done"), sem("rden_done")
        prob_done, wgt_done, c_ready, c_out = sem("prob_done"), sem("wgt_done"), sem("c_ready"), sem("c_out")
        act_done, f_ready, f_out = sem("act_done"), sem("f_ready"), sem("f_out")
        sel_step, rank_out, rankT_ready, rankT_out, pick_done = (
            sem(n) for n in ("sel_step", "rank_out", "rankT_ready", "rankT_out", "pick_done"))
        gate_exp, gate_step = sem("gate_exp"), sem("gate_step")
        s_ready, s_masked, max_done, p_exp, rinv_done, rgate_done, p_scaled = (
            sem(n) for n in ("s_ready", "s_masked", "max_done", "p_exp", "rinv_done", "rgate_done", "p_scaled"))
        out_ready, stats2, mean2, norm2_ready, s_done = (
            sem(n) for n in ("out_ready", "stats2", "mean2", "norm2_ready", "s_done"))
        y_step, y_done, y_stored = sem("y_step"), sem("y_done"), sem("y_stored")

        M_UNITS = 12
        (U_QW, U_KW, U_VW, U_COMP, U_SEL, U_SELT, U_QK, U_V,
         U_VWW, U_VWC, U_PTW, U_PTC) = range(M_UNITS)

        def m_unit(b, k):
            return M_UNITS * b + k

        x_v = x.rearrange("b (t p) d -> p (b t) d", p=P)
        out_v = out.rearrange("b (t p) d -> p (b t) d", p=P)

        CONSTS = 4 + WPT

        passed = {e: sem(f"passed_{i}") for i, e in enumerate(nc.engines)}

        def wait_reg(eng, signal, value):
            eng.wait_ge(signal, value)
            if not isinstance(value, int):
                eng.sem_inc(passed[eng.engine], 1)

        def load_experts(eng, dst, src, signal):
            for i0, rows, length, at in RUNS:
                part = src[i0 * TOPK:(i0 + rows) * TOPK, :].rearrange("(i j) d -> i j d", j=TOPK)[:, 0:length, :]
                eng.dma_start(dst[at:at + rows * length, :], part).then_inc(signal, 16)

        block = ctx.enter_context(nc.Block())

        @block.sync
        def _(sp):
            for i, (t0, t1) in enumerate(((0, TB), (TB, 2 * TB), (2 * TB, TILES))):
                sp.dma_start(x_sb[:, t0:t1, :], x_v[:, t0:t1, :]).then_inc(x_in[i], 16)
            for dst, src in ((wq_sb, wq), (wk_sb, wk), (wv_sb, wv)):
                sp.dma_start(dst[:, :], src[:, :]).then_inc(w_late, 16)
            for dst, src in ((bq_sb, bq), (bk_sb, bk), (bv_sb, bv), (bc_sb, bc)):
                sp.dma_start(dst[:, :], src.rearrange("(n a) -> n a", a=1)).then_inc(w_late, 16)
            sp.dma_start(wc_sb[:, :, :], wc.rearrange("(r p) n -> p r n", p=P)).then_inc(w_late, 16)
            sp.dma_start(wo_sb[:, :, :], wo.rearrange("(r p) n -> p r n", p=P)).then_inc(w_late, 16)
            sp.dma_start(bo_row[:, :], bo.rearrange("(a n) -> a n", a=1)).then_inc(w_late, 16)
            load_experts(sp, up_sb, ffn_up, w_late)

            def load_tiles(b, reload=True):
                for j in range(TB):
                    if reload:
                        sp.wait_ge(sim_ready, TB * (b - 1) + j + 1)
                    sp.dma_start(xTc[:, j, :], xT_all[:, bass.ds((TB * b + j) * P, P)]).then_inc(tile_in[j], 16)

            sp.wait_ge(xt_out, 1)
            load_tiles(0, reload=False)
            sp.wait_ge(z_out, B)
            sp.dma_start(sc8[:, :], zT_all[0:1, :].rearrange("a (b l) -> a b l", b=B)).then_inc(sc8_in, 16)

            def store_y(b):
                sp.wait_ge(y_done, b + 1)
                sp.dma_start(out_v[:, bass.ts(b, TB), :], y_sb[:, :, :]).then_inc(y_stored, 16)

            sp.wait_ge(rank_out, 1)
            sp.dma_start(rank32[:, :], sel_rank[:, :].rearrange("b (t l) -> b t l", t=TB)).then_inc(y_stored, 16)
            load_tiles(1)
            with sp.Fori(2, B) as b:
                load_tiles(b)
                store_y(b - 2)
            store_y(B - 2)
            store_y(B - 1)
            sp.wait_ge(y_stored, 16 * (B + 1))

        @block.gpsimd
        def _(pool):
            steps = [0]

            def step(ins):
                steps[0] += 1
                ins.then_inc(consts, 1)
                pool.wait_ge(consts, steps[0])

            step(nc.gpsimd.memset(ident[:, :], 0.0))
            step(nc.gpsimd.affine_select(out=ident[:, :], in_=ident[:, :], compare_op=ALU.not_equal, fill=1.0,
                                         base=0, pattern=[[-1, P]], channel_multiplier=1))
            nc.gpsimd.memset(neg_half[:, :], -0.5)
            nc.gpsimd.memset(ones_row[:, :], 1.0)
            nc.gpsimd.memset(zero_row[:, :], 0.0)
            nc.gpsimd.memset(rsum[:, :], 1.0)
            nc.gpsimd.memset(pT_cs[:, :, :], 0.0)
            step(nc.gpsimd.memset(win_mask[:, :], TAKEN))
            for w in range(WPT):
                step(nc.gpsimd.memset(win_mask[w * WINDOW:(w + 1) * WINDOW, w * STEP_W:w * STEP_W + WINDOW], 0.0))
            step(nc.gpsimd.iota(rank_row[:, :], pattern=[[1, SELECT_K]], base=1, channel_multiplier=0,
                                allow_small_or_imprecise_dtypes=True))

            def norm_terms(mv, eps, var, rstd, prod, nmr, before, done):
                nc.gpsimd.tensor_scalar(var[:, :], mv[:, :, 1], eps, None, ALU.add).then_inc(pool_step, 1)
                pool.wait_ge(pool_step, before + 1)
                nc.gpsimd.tensor_tensor(rstd[:, :], var[:, :], neg_half[:, :], ALU.pow).then_inc(pool_step, 1)
                pool.wait_ge(pool_step, before + 2)
                nc.gpsimd.tensor_tensor(prod[:, :], mv[:, :, 0], rstd[:, :], ALU.mult).then_inc(pool_step, 1)
                wait_reg(pool, pool_step, before + 3)
                nc.gpsimd.tensor_scalar(nmr[:, :], prod[:, :], -1.0, None, ALU.mult).then_inc(done, 1)

            def norm1_pair(p, first=False):
                for s in range(2):
                    b = 2 * p + s
                    if not first:
                        pool.wait_ge(xn_done, b - 1)
                    wait_reg(pool, mean1, b + 1)
                    norm_terms(mv1[s], 1e-5, var1[s], rstd1[s], prod1[s], nmr1[s], 3 * b, norm1_ready)

            norm1_pair(0, first=True)
            with pool.Fori(1, B // 2) as p:
                norm1_pair(p)

            def build_cands(n, j, first):
                d = j % 2
                pool.wait_ge(top_done, 2 * n + 2)
                if not (first and n < 1):
                    pool.wait_ge(cand_ready, n)
                nc.gpsimd.tensor_tensor(shifted[:, :, :], top[d][:, :, :],
                                        top[d][:, :, 0:1].to_broadcast([P, VECS, TOPK]),
                                        ALU.subtract).then_inc(shift_done, 1)
                pool.wait_ge(shift_done, n + 1)
                if not (first and n < 2):
                    pool.wait_ge(left_done, 2 * n - 2)
                    pool.wait_ge(exp_done, n - 1)
                for i0, rows, length, at in RUNS:
                    o = cand[d][:, :, at:at + rows * length].rearrange("p h (i j) -> p h i j", i=rows)
                    a = shifted[:, 0:HEADS, i0:i0 + rows].unsqueeze(3).to_broadcast([P, HEADS, rows, length])
                    c = shifted[:, HEADS:VECS, 0:length].unsqueeze(2).to_broadcast([P, HEADS, rows, length])
                    last = nc.gpsimd.tensor_tensor(o, a, c, ALU.add)
                last.then_inc(cand_ready, 1)

            def weigh(n, j, first=False):
                d = j % 2
                pool.wait_ge(exp_done, n + 1)
                if not (first and n < 1):
                    pool.wait_ge(wgt_done, n)
                nc.gpsimd.tensor_tensor(prob[:, :, :], e_all[d][:, :, :], e_left[d][:, :, :],
                                        ALU.subtract).then_inc(prob_done, 1)
                pool.wait_ge(prob_done, n + 1)
                pool.wait_ge(rden_done, n + 1)
                if not (first and n < 2):
                    pool.wait_ge(c_ready, n - 1)
                nc.gpsimd.tensor_tensor(wgt[d][:, :, :], prob[:, :, :],
                                        rden[d][:, :].unsqueeze(2).to_broadcast([P, HEADS, CANDS]),
                                        ALU.mult).then_inc(wgt_done, 1)

            def gelu_times_weights(b):
                pool.wait_ge(c_out, b + 1)
                nc.gpsimd.tensor_tensor(actT[:, :], geluT[:, bass.ts(b, L)], c_sb[:, :],
                                        ALU.mult).then_inc(act_done, 1)

            def scale_probs(b):
                pool.wait_ge(rinv_done, b + 1)
                nc.gpsimd.tensor_tensor(rgate[:, 0:TB], rinv[:, 0:TB], gates[:, bass.ts(b, TB), WIN], ALU.mult)
                nc.gpsimd.tensor_tensor(rgate[:, TB:TB + 2], rinv[:, TB:TB + 2],
                                        gates[:, bass.ds(b * TB, 1), COMP:SEL + 1].rearrange("p a g -> p (a g)"),
                                        ALU.mult).then_inc(rgate_done, 1)
                pool.wait_ge(rgate_done, b + 1)
                nc.gpsimd.tensor_tensor(p_win[:, :, :], p_win[:, :, :],
                                        rgate[:, 0:TB].unsqueeze(2).to_broadcast([P, TB, WKEYS]), ALU.mult)
                nc.gpsimd.tensor_tensor(p_cs[:, 0:BLOCKS], p_cs[:, 0:BLOCKS],
                                        rgate[:, TB:TB + 1].to_broadcast([P, BLOCKS]), ALU.mult)
                nc.gpsimd.tensor_tensor(p_cs[0:SELECT_K, BLOCKS:CS], p_cs[0:SELECT_K, BLOCKS:CS],
                                        rgate[0:SELECT_K, TB + 1:TB + 2].to_broadcast([SELECT_K, SELECT_K]),
                                        ALU.mult).then_inc(p_scaled, 1)

            def norm2(b):
                wait_reg(pool, mean2, b + 1)
                norm_terms(mv2, 4e-6, var2, rstd2, prod2, nmr2, 3 * B + 3 * b, norm2_ready)

            def finish_rows(b):
                pool.wait_ge(f_out, b + 1)
                nc.gpsimd.tensor_tensor(y1[:, :, :], half_f[:, :, :], tanh_f[:, :, :], ALU.mult).then_inc(y_step, 1)
                pool.wait_ge(y_step, 3 * b + 1)
                nc.gpsimd.tensor_tensor(y2[:, :, :], y1[:, :, :], half_f[:, :, :], ALU.add).then_inc(y_step, 1)
                pool.wait_ge(y_step, 3 * b + 2)
                pool.wait_ge(s_done, b + 1)
                nc.gpsimd.tensor_tensor(y3[:, :, :], y2[:, :, :], s_norm[:, :, :], ALU.mult).then_inc(y_step, 1)
                pool.wait_ge(y_step, 3 * b + 3)
                pool.wait_ge(y_stored, 16 * (b + 1))
                nc.gpsimd.tensor_tensor(y_sb[:, :, :], y3[:, :, :], x_sb[:, bass.ts(b, TB), :],
                                        ALU.add).then_inc(y_done, 1)

            def body(b, first=False):
                for j in range(TB):
                    n = TB * b + j
                    if j == TB - 1 and not first:
                        scale_probs(b)
                    if not (first and n < 2):
                        weigh(n - 2, j, first)
                    if j == 2 and not first:
                        gelu_times_weights(b - 1)
                    build_cands(n, j, first)
                    if j == 0 and not first:
                        norm2(b - 1)
                    if j == TB - 1 and not first:
                        finish_rows(b - 1)
                    if j == TB - 1 and first:
                        scale_probs(b)

            body(0, first=True)
            with pool.Fori(1, B) as b:
                body(b)
            weigh(TILES - 2, 0)
            norm2(B - 1)
            weigh(TILES - 1, 1)
            gelu_times_weights(B - 1)
            finish_rows(B - 1)

        @block.scalar
        def _(act):
            act.dma_start(keys_sb[:, :, :], ffn_keys.rearrange("(t h) k s c -> (h k) t (s c)", t=2)).then_inc(w_ffn, 16)
            for half in range(2):
                act.dma_start(fwq_sb[half * DKEY:(half + 1) * DKEY, :, :],
                              ffn_wq[bass.ts(half, HEADS * DKEY), :].rearrange("(h c) d -> c h d", h=HEADS)
                              ).then_inc(w_ffn, 16)
            load_experts(act, down_sb, ffn_down, w_ffn)
            act.dma_start(wz_sb[:, 0:1], ws[:, :]).then_inc(w_att, 16)
            act.dma_start(wz_sb[:, 1:4], wg[:, :]).then_inc(w_att, 16)
            act.dma_start(bz_sb[0:1, :], bs.rearrange("(n a) -> n a", a=1)).then_inc(w_att, 16)
            act.dma_start(bz_sb[1:4, :], bg.rearrange("(n a) -> n a", a=1)).then_inc(w_att, 16)
            act.wait_ge(w_att, 16 * W_ATT)

            def norm_rows(b, s):
                act.wait_ge(norm1_ready, b + 1)
                for j in range(TB):
                    t = bass.ds(TB * b + j, 1)
                    last = nc.scalar.activation(xn_all[:, t, :].rearrange("p a d -> p (a d)"),
                                                x_sb[:, t, :].rearrange("p a d -> p (a d)"), ACT.Identity,
                                                bias=nmr1[s][:, j:j + 1], scale=rstd1[s][:, j:j + 1])
                last.then_inc(xn_done, 1)

            def take_out(b, s):
                act.wait_ge(xt_full, b + 1)
                nc.scalar.activation(xT_all[:, bass.ts(b, L)], scratch[s][:, :], ACT.Copy).then_inc(xt_out, 1)
                act.wait_ge(h_full, b + 1)
                nc.scalar.activation(geluT[:, bass.ts(b, L)], h_bank[s][0:CANDS, :], ACT.Gelu).then_inc(gelu_done, 1)
                act.wait_ge(z_full, b + 1)
                nc.scalar.activation(zT_all[:, bass.ts(b, L)], f_bank[0:4, :], ACT.Identity,
                                     bias=bz_sb[:, 0:1]).then_inc(z_out, 1)

            norm_rows(0, 0)
            norm_rows(1, 1)
            with act.Fori(0, B // 2 - 1) as p:
                take_out(2 * p, 0)
                norm_rows(2 * p + 2, 0)
                take_out(2 * p + 1, 1)
                norm_rows(2 * p + 3, 1)
            take_out(B - 2, 0)
            take_out(B - 1, 1)
            act.wait_ge(w_late, 16 * W_LATE)
            nc.scalar.activation(bqs_sb[:, :], bq_sb[:, :], ACT.Copy, scale=SCALE).then_inc(bqs_done, 1)
            act.wait_ge(bqs_done, 1)
            act.wait_ge(zg_full, 1)
            nc.scalar.activation(gexp[:, :, :], s_bank[:, 0:4 * TILES].rearrange("p (t g) -> p t g", g=4)[:, :, 1:4],
                                 ACT.Exp, scale=-1.0).then_inc(gate_exp, 1)

            def exps(n, j, first=False):
                d = j % 2
                act.wait_ge(best_done, 2 * n + 2)
                if not (first and n < 2):
                    act.wait_ge(rden_done, n - 1)
                nc.scalar.activation(e_best[d][:, :, :], best[d][:, :, :], ACT.Exp).then_inc(exp_best, 1)
                if not (first and n < 2):
                    act.wait_ge(wgt_done, n - 1)
                nc.scalar.activation(e_all[d][:, :, :], cand[d][:, :, :], ACT.Exp)
                act.wait_ge(left_done, 2 * n + 2)
                nc.scalar.activation(e_left[d][:, :, :], left[d][:, :, :], ACT.Exp).then_inc(exp_done, 1)

            def unit(b, k, outs):
                act.wait_ge(unit_full, m_unit(b, k) + 1)
                for dst, cols, bias, scale in outs:
                    src = scratch[k % 2][0:dst.shape[0], cols:cols + dst.shape[1]]
                    if bias is None:
                        last = nc.scalar.activation(dst, src, ACT.Copy)
                    else:
                        last = nc.scalar.activation(dst, src, ACT.Identity, bias=bias[:, 0:1], scale=scale)
                last.then_inc(unit_out, 1)

            def norm_attention(b):
                act.wait_ge(norm2_ready, b + 1)
                for j in range(TB):
                    last = nc.scalar.activation(s_norm[:, j, :], out_bank[:, bass.ts(j, D)], ACT.Identity,
                                                bias=nmr2[:, j:j + 1], scale=rstd2[:, j:j + 1])
                last.then_inc(s_done, 1)

            def weights_out(b):
                act.wait_ge(c_ready, TB * b + TB)
                nc.scalar.activation(c_sb[:, :], c_bank[0:CANDS, :], ACT.Copy).then_inc(c_out, 1)

            def silu_parts(b):
                act.wait_ge(f_ready, b + 1)
                f_v = f_bank[:, :].rearrange("p (t d) -> p t d", t=TB)
                nc.scalar.activation(tanh_f[:, :, :], f_v, ACT.Tanh, scale=0.5)
                nc.scalar.activation(half_f[:, :, :], f_v, ACT.Copy, scale=0.5).then_inc(f_out, 1)

            def body(b, first=False):
                for j in range(TB):
                    n = TB * b + j
                    if first and j == 1:
                        exps(0, 0, True)
                    elif not (first and j < 3):
                        exps(n - 2, j, first)
                    if j == 0:
                        act.wait_ge(unit_full, m_unit(b, U_QW) + 1)
                        overlap = bass.AP(scratch[U_QW % 2], 0, [[512, P], [STEP_W, L // WINDOW], [1, WINDOW]])
                        nc.scalar.activation(qw[:, :].rearrange("p (w t) -> p w t", t=WINDOW), overlap, ACT.Identity,
                                             bias=bqs_sb[:, 0:1], scale=SCALE).then_inc(unit_out, 1)
                        unit(b, U_KW, [(kw[:, :], 0, bk_sb, 1.0)])
                        unit(b, U_VW, [(vw[:, :], 0, bv_sb, 1.0)])
                        unit(b, U_COMP, [(csT[:, 0:BLOCKS], 0, bc_sb, 1.0)])
                    if j == 1:
                        if not first:
                            norm_attention(b - 1)
                        unit(b, U_SEL, [(xsel[:, :], 0, None, 1.0)])
                        unit(b, U_SELT, [(csT[:, BLOCKS:CS], 0, None, 1.0)])
                        unit(b, U_QK, [(qcs[:, :], 0, bqs_sb, SCALE), (kcs[:, :], CS, bk_sb, 1.0)])
                        unit(b, U_V, [(vcs[:, :], 0, bv_sb, 1.0)])
                    if j == 2:
                        if not first:
                            weights_out(b - 1)
                        unit(b, U_VWW, [(vww[:, :, :].rearrange("p t d -> p (t d)"), 0, None, 1.0)])
                        unit(b, U_VWC, [(vwc[:, :, :].rearrange("p t d -> p (t d)"), 0, None, 1.0)])
                    if j == (3 if first else 2):
                        act.wait_ge(max_done, b + 1)
                        for g in range(TB):
                            nc.scalar.activation(p_win[:, g, :], s_win[:, g, :], ACT.Exp,
                                                 bias=nmax[:, g:g + 1], accum_out=rsum[:, g:g + 1])
                        nc.scalar.activation(p_cs[:, 0:BLOCKS], s_bank[:, TB * WKEYS:TB * WKEYS + BLOCKS], ACT.Exp,
                                             bias=nmax[:, TB:TB + 1], accum_out=rsum[:, TB:TB + 1])
                        nc.scalar.activation(p_cs[0:SELECT_K, BLOCKS:CS],
                                             s_bank[0:SELECT_K, TB * WKEYS + BLOCKS:TB * WKEYS + CS], ACT.Exp,
                                             bias=nmax[0:SELECT_K, TB + 1:TB + 2],
                                             accum_out=rsum[0:SELECT_K, TB + 1:TB + 2]).then_inc(p_exp, 1)
                    if j == 3:
                        if not first:
                            silu_parts(b - 1)
                        unit(b, U_PTW, [(pT_win[:, :, :].rearrange("p t q -> p (t q)"), 0, None, 1.0)])
                        unit(b, U_PTC, [(pT_cs[:, 0, :], 0, None, 1.0),
                                        (pT_cs[0:SELECT_K, 1, 0:SELECT_K], P, None, 1.0)])

            body(0, first=True)
            with act.Fori(1, B) as b:
                body(b)
            exps(TILES - 2, 0)
            norm_attention(B - 1)
            exps(TILES - 1, 1)
            weights_out(B - 1)
            silu_parts(B - 1)

        @block.vector
        def _(dve):
            def stats_of(src, st, mv, counter, before, done):
                for j in range(TB):
                    last = nc.vector.bn_stats(st[:, j, :], src(j))
                last.then_inc(counter, 1)
                wait_reg(dve, counter, before + 1)
                for j in range(TB):
                    last = nc.vector.bn_aggr(mv[:, j, :], st[:, j, :])
                last.then_inc(done, 1)

            def prologue_pair(p, first=False):
                for s in range(2):
                    b = 2 * p + s
                    if first:
                        dve.wait_ge(x_in[s], 16)
                    else:
                        dve.wait_ge(norm1_ready, b - 1)
                    stats_of(lambda j: x_sb[:, bass.ds(TB * b + j, 1), :].rearrange("p a d -> p (a d)"),
                             st1[s], mv1[s], stats1, b, mean1)

            prologue_pair(0, first=True)
            dve.wait_ge(prep_pe, 1)
            nc.vector.tensor_copy(keysT[:, :], f_bank[:, 0:HK])
            nc.vector.tensor_copy(downT[:, :], c_bank[:, 0:CANDS]).then_inc(prep_dve, 1)
            dve.wait_ge(x_in[2], 16)
            with dve.Fori(1, B // 2) as p:
                prologue_pair(p)
            dve.wait_ge(prep_pe, 2)
            nc.vector.tensor_copy(sim_w[:, 0:HK], sim_bank[0][:, 0:HK])
            nc.vector.tensor_copy(sim_w[:, HK:2 * HK], sim_bank[1][:, 0:HK]).then_inc(prep_dve, 1)

            def denominators(n, j, first):
                d = j % 2
                if not (first and n < 1):
                    dve.wait_ge(rden_done, n)
                dve.wait_ge(exp_best, n + 1)
                nc.vector.tensor_reduce(den[:, :], e_best[d][:, :, :], AX_X, ALU.add).then_inc(den_done, 1)
                dve.wait_ge(den_done, n + 1)
                if not (first and n < 2):
                    dve.wait_ge(wgt_done, n - 1)
                nc.vector.reciprocal(rden[d][:, :], den[:, :]).then_inc(rden_done, 1)

            def sort_scores(n, j, first=False, tail=None):
                d = j % 2
                if not (first and n < 2):
                    dve.wait_ge(shift_done, n - 1)
                wait_reg(dve, sim_ready, n + 1)
                for h in range(2):
                    for v in range(h * HALF_V, (h + 1) * HALF_V):
                        last = nc.vector.max(top[d][:, v, 0:8], sim_bank[d][:, bass.ts(v, KEYS)])
                    last.then_inc(sim_top8, 1)
                if tail is not None:
                    tail()
                for h in range(2):
                    if not (first and n < 1):
                        dve.wait_ge(top_done, 2 * n - 1 + h)
                    wait_reg(dve, sim_top8, 2 * n + 1 + h)
                    for v in range(h * HALF_V, (h + 1) * HALF_V):
                        last = nc.vector.match_replace(out=rest[:, v, :], in_to_replace=top[d][:, v, 0:8],
                                                       in_values=sim_bank[d][:, bass.ts(v, KEYS)],
                                                       imm_value=NO_SCORE)
                    last.then_inc(sim_used, 1)
                for h in range(2):
                    wait_reg(dve, sim_used, 2 * n + 1 + h)
                    for v in range(h * HALF_V, (h + 1) * HALF_V):
                        last = nc.vector.max(top[d][:, v, 8:16], rest[:, v, :])
                    last.then_inc(top_done, 1)

            def take_best(n, j, first=False):
                d = j % 2
                halves = [range(h * HALF_H, (h + 1) * HALF_H) for h in range(2)]
                if not (first and n < 2):
                    dve.wait_ge(exp_best, n - 1)
                wait_reg(dve, cand_ready, n + 1)
                for hs in halves:
                    for h in hs:
                        last = nc.vector.max(best[d][:, h, 0:8], cand[d][:, h, :])
                    last.then_inc(best8, 1)
                if not (first and n < 1):
                    dve.wait_ge(left_done, 2 * n)
                for k, hs in enumerate(halves):
                    wait_reg(dve, best8, 2 * n + 1 + k)
                    for h in hs:
                        last = nc.vector.match_replace(out=crest[:, h, :], in_to_replace=best[d][:, h, 0:8],
                                                       in_values=cand[d][:, h, :], imm_value=TAKEN)
                    last.then_inc(best8_out, 1)
                for k, hs in enumerate(halves):
                    wait_reg(dve, best8_out, 2 * n + 1 + k)
                    for h in hs:
                        last = nc.vector.max(best[d][:, h, 8:16], crest[:, h, :])
                    last.then_inc(best_done, 1)
                if not (first and n < 2):
                    dve.wait_ge(exp_done, n - 1)
                for k, hs in enumerate(halves):
                    wait_reg(dve, best_done, 2 * n + 1 + k)
                    for h in hs:
                        last = nc.vector.match_replace(out=left[d][:, h, :], in_to_replace=best[d][:, h, 8:16],
                                                       in_values=crest[:, h, :], imm_value=TAKEN)
                    last.then_inc(left_done, 1)

            def chain(n_done, ins):
                ins.then_inc(sel_step, 1)
                dve.wait_ge(sel_step, n_done)

            def select_tokens():
                dve.wait_ge(sc8_in, 16)
                k = 0
                src, dst = sc8, sel_a
                for r in range(SELECT_K // 8):
                    k += 1
                    chain(k, nc.vector.max(sel_m[:, :], src[:, :]))
                    k += 1
                    chain(k, nc.vector.match_replace(out=dst[:, :], in_to_replace=sel_m[:, :],
                                                     in_values=src[:, :], imm_value=NO_SCORE))
                    src, dst = dst, (sel_b if dst is sel_a else sel_a)
                k += 1
                chain(k, nc.vector.tensor_scalar(sel_mask[:, :], src[:, :], NO_SCORE, None, ALU.is_equal))
                k += 1
                chain(k, nc.vector.tensor_tensor_scan(sel_cnt[:, :], sel_mask[:, :], zero_row[0:B, :], 0.0,
                                                      ALU.add, ALU.add))
                nc.vector.tensor_tensor(sel_rank[:, :], sel_cnt[:, :], sel_mask[:, :], ALU.mult).then_inc(rank_out, 1)

            def normalise_gates():
                dve.wait_ge(gate_exp, 1)
                k = [0]

                def link(ins):
                    k[0] += 1
                    ins.then_inc(gate_step, 1)
                    dve.wait_ge(gate_step, k[0])

                link(nc.vector.tensor_scalar(gexp[:, :, :], gexp[:, :, :], 1.0, None, ALU.add))
                link(nc.vector.reciprocal(gsig[:, :, :], gexp[:, :, :]))
                link(nc.vector.tensor_reduce(gsum[:, :], gsig[:, :, :], AX_X, ALU.add))
                link(nc.vector.tensor_scalar(gsum[:, :], gsum[:, :], 1e-6, None, ALU.add))
                link(nc.vector.reciprocal(gsum[:, :], gsum[:, :]))
                link(nc.vector.tensor_tensor(gates[:, :, :], gsig[:, :, :],
                                             gsum[:, :].unsqueeze(2).to_broadcast([P, TILES, 3]), ALU.mult))

            def pick_matrix(b):
                for j in range(TB):
                    last = nc.vector.tensor_scalar(pick[:, j, :], rank_row[:, :],
                                                   rankT[:, bass.ds(TB * b + j, 1)], None, ALU.is_equal)
                last.then_inc(pick_done, 1)

            def maxima(b):
                dve.wait_ge(s_ready, b + 1)
                nc.vector.tensor_tensor(s_win[:, :, :], s_bank[:, 0:TB * WKEYS].rearrange("p (g k) -> p g k", g=TB),
                                        win_mask[:, :].unsqueeze(1).to_broadcast([P, TB, WKEYS]),
                                        ALU.add).then_inc(s_masked, 1)
                nc.vector.tensor_reduce(nmax[:, TB:TB + 1], s_bank[:, TB * WKEYS:TB * WKEYS + BLOCKS], AX_X, ALU.max,
                                        negate=True)
                nc.vector.tensor_reduce(nmax[0:SELECT_K, TB + 1:TB + 2],
                                        s_bank[0:SELECT_K, TB * WKEYS + BLOCKS:TB * WKEYS + CS], AX_X, ALU.max,
                                        negate=True)
                dve.wait_ge(s_masked, b + 1)
                nc.vector.tensor_reduce(nmax[:, 0:TB], s_win[:, :, :], AX_X, ALU.max, negate=True).then_inc(max_done, 1)

            def norm2_stats(b):
                dve.wait_ge(out_ready, b + 1)
                stats_of(lambda j: out_bank[:, bass.ts(j, D)], st2, mv2, stats2, b, mean2)

            def body(b, first=False):
                for j in range(TB):
                    n = TB * b + j
                    tail = (lambda: denominators(n - 2, j, first)) if not (first and n < 2) else None
                    sort_scores(n, j, first, tail)
                    if first and j == 2:
                        normalise_gates()
                        dve.wait_ge(rankT_ready, 1)
                        nc.vector.tensor_copy(rankT[:, :], f_bank[:, 0:TILES]).then_inc(rankT_out, 1)
                        dve.wait_ge(rankT_out, 1)
                        pick_matrix(0)
                    if j == 0 and not first:
                        norm2_stats(b - 1)
                    if j == (3 if first else 2):
                        maxima(b)
                    if not (first and n < 1):
                        take_best(n - 1, j - 1, first)
                    if first and j == 1:
                        dve.wait_ge(consts, CONSTS)
                        select_tokens()
                    if j == 0 and not first:
                        pick_matrix(b)
                    if j == (3 if first else 2):
                        dve.wait_ge(p_exp, b + 1)
                        nc.vector.reciprocal(rinv[:, :], rsum[:, :]).then_inc(rinv_done, 1)

            body(0, first=True)
            with dve.Fori(1, B) as b:
                body(b)
            denominators(TILES - 2, 0, False)
            norm2_stats(B - 1)
            take_best(TILES - 1, 1)
            denominators(TILES - 1, 1, False)

        @block.tensor
        def _(pe):
            mm = nc.tensor.matmul

            pe.wait_ge(consts, CONSTS)
            pe.wait_ge(w_ffn, 16 * W_FFN)
            for t in range(2):
                nc.tensor.transpose(f_bank[:, bass.ts(t, P)], keys_sb[:, t, :], ident[:, :])
            nc.tensor.transpose(c_bank[:, 0:CANDS], down_sb[:, :], ident[0:CANDS, 0:CANDS]).then_inc(prep_pe, 1)
            pe.wait_ge(prep_dve, 1)
            for half, dst in enumerate(sim_bank):
                for h in range(HEADS):
                    last = mm(dst[:, bass.ts(h, KEYS)], fwq_sb[half * DKEY:(half + 1) * DKEY, h, :],
                              keysT[half * DKEY:(half + 1) * DKEY, bass.ts(h, KEYS)], start=True, stop=True)
            last.then_inc(prep_pe, 1)

            def fill(u, parity, after=None):
                if not (isinstance(u, int) and u < 2):
                    wait_reg(pe, unit_out, u - 1)
                if after is not None:
                    wait_reg(pe, unit_out, after + 1)
                return scratch[parity]

            def transpose_rows(b):
                pe.wait_ge(xn_done, b + 1)
                if b >= 2:
                    pe.wait_ge(xt_out, b - 1)
                for j in range(TB):
                    last = nc.tensor.transpose(scratch[b % 2][:, bass.ts(j, P)], xn_all[:, TB * b + j, :], ident[:, :])
                last.then_inc(xt_full, 1)

            def logits(b):
                rows = xT_all[:, bass.ts(b, L)]
                pe.wait_ge(xt_out, b + 1)
                if b >= 2:
                    pe.wait_ge(gelu_done, b - 1)
                mm(h_bank[b % 2][0:CANDS, :], downT[:, :], rows, start=True, stop=True).then_inc(h_full, 1)
                if b >= 1:
                    pe.wait_ge(z_out, b)
                    gate_columns(b - 1)
                mm(f_bank[0:4, :], wz_sb[:, :], rows, start=True, stop=True).then_inc(z_full, 1)

            def gate_columns(b):
                for j in range(TB):
                    t = TB * b + j
                    last = nc.tensor.transpose(s_bank[:, bass.ts(t, 4)], zT_all[:, bass.ts(t, P)], ident[0:4, 0:4])
                return last

            def scores(n, j, b, first=False):
                pe.wait_ge(tile_in[j], 16 * (b + 1))
                if not (first and n < 2):
                    pe.wait_ge(sim_used, 2 * n - 2)
                mm(sim_bank[j % 2][:, :], xTc[:, j, :], sim_w[:, :], start=True, stop=True).then_inc(sim_ready, 1)

            def expert_weights(n, j, first=False):
                d = j % 2
                pe.wait_ge(wgt_done, n + 1)
                for h in range(HEADS):
                    last = mm(c_bank[0:CANDS, bass.ts(j, P)], wgt[d][:, h, :], ident[:, :],
                              start=(h == 0), stop=(h == HEADS - 1))
                last.then_inc(c_ready, 1)

            def experts_out(b):
                pe.wait_ge(act_done, b + 1)
                for j in range(TB):
                    last = mm(f_bank[:, bass.ts(j, D)], actT[:, bass.ts(j, P)], up_sb[:, :], start=True, stop=True)
                last.then_inc(f_ready, 1)

            def project_windows(b):
                for k, w in ((U_QW, wq_sb), (U_KW, wk_sb), (U_VW, wv_sb)):
                    o = fill(m_unit(b, k), k % 2)
                    mm(o[:, 0:WTOK], w[:, :], xT_all[:, bass.ds(b * L, WTOK)],
                       start=True, stop=True).then_inc(unit_full, 1)
                o = fill(m_unit(b, U_COMP), U_COMP % 2)
                rows = xT_all[:, bass.ts(b, L)].rearrange("p (c r) -> p r c", r=RATIO)
                for r in range(RATIO):
                    last = mm(o[:, 0:BLOCKS], wc_sb[:, r, :], rows[:, r, :], start=(r == 0), stop=(r == RATIO - 1))
                last.then_inc(unit_full, 1)

            def project_selected(b):
                pe.wait_ge(pick_done, b + 1)
                o = fill(m_unit(b, U_SEL), U_SEL % 2)
                for j in range(TB):
                    last = mm(o[0:SELECT_K, 0:D], pick[:, j, :],
                              xn_all[:, bass.ds(b * TB + j, 1), :].rearrange("p a d -> p (a d)"),
                              start=(j == 0), stop=(j == TB - 1))
                last.then_inc(unit_full, 1)
                o = fill(m_unit(b, U_SELT), U_SELT % 2, m_unit(b, U_SEL))
                nc.tensor.transpose(o[:, 0:SELECT_K], xsel[:, :], ident[0:SELECT_K, 0:SELECT_K]).then_inc(unit_full, 1)
                o = fill(m_unit(b, U_QK), U_QK % 2, m_unit(b, U_SELT))
                mm(o[:, 0:CS], wq_sb[:, :], csT[:, :], start=True, stop=True)
                mm(o[:, CS:2 * CS], wk_sb[:, :], csT[:, :], start=True, stop=True).then_inc(unit_full, 1)
                o = fill(m_unit(b, U_V), U_V % 2)
                mm(o[:, 0:CS], wv_sb[:, :], csT[:, :], start=True, stop=True).then_inc(unit_full, 1)

            def attention_scores(b, first=False):
                pe.wait_ge(unit_out, m_unit(b, U_QK) + 1)
                if first:
                    pe.wait_ge(gate_exp, 1)
                else:
                    pe.wait_ge(p_exp, b)
                for g in range(TB):
                    k0 = g * WPT * STEP_W
                    mm(s_bank[:, bass.ts(g, WKEYS)], qw[:, bass.ts(g, P)], kw[:, k0:k0 + WKEYS], start=True, stop=True)
                c0 = TB * WKEYS
                mm(s_bank[:, c0:c0 + BLOCKS], qcs[:, 0:BLOCKS], kcs[:, 0:BLOCKS], start=True, stop=True)
                mm(s_bank[0:SELECT_K, c0 + BLOCKS:c0 + CS], qcs[:, BLOCKS:CS], kcs[:, BLOCKS:CS],
                   start=True, stop=True).then_inc(s_ready, 1)

            def values_out(b):
                o = fill(m_unit(b, U_VWW), U_VWW % 2, m_unit(b, U_V))
                for g in range(TB):
                    k0 = g * WPT * STEP_W
                    last = mm(o[0:WKEYS, bass.ts(g, D)], vw[:, k0:k0 + WKEYS], wo_sb[:, WIN, :], start=True, stop=True)
                last.then_inc(unit_full, 1)
                o = fill(m_unit(b, U_VWC), U_VWC % 2)
                mm(o[:, 0:D], vcs[:, 0:BLOCKS], wo_sb[:, COMP, :], start=True, stop=True)
                mm(o[0:SELECT_K, D:2 * D], vcs[:, BLOCKS:CS], wo_sb[:, SEL, :], start=True, stop=True).then_inc(unit_full, 1)

            def attention_out(b, first=False):
                pe.wait_ge(p_scaled, b + 1)
                o = fill(m_unit(b, U_PTW), U_PTW % 2)
                for g in range(TB):
                    last = nc.tensor.transpose(o[0:WKEYS, bass.ts(g, P)], p_win[:, g, :], ident[:, :])
                last.then_inc(unit_full, 1)
                o = fill(m_unit(b, U_PTC), U_PTC % 2)
                nc.tensor.transpose(o[:, 0:P], p_cs[:, 0:BLOCKS], ident[:, :])
                nc.tensor.transpose(o[0:SELECT_K, P:P + SELECT_K], p_cs[0:SELECT_K, BLOCKS:CS],
                                    ident[0:SELECT_K, 0:SELECT_K]).then_inc(unit_full, 1)
                pe.wait_ge(unit_out, m_unit(b, U_PTC) + 1)
                if not first:
                    pe.wait_ge(s_done, b)
                for j in range(TB):
                    o = out_bank[:, bass.ts(j, D)]
                    mm(o, ident[:, :], xn_all[:, bass.ds(b * TB + j, 1), :].rearrange("p a d -> p (a d)"),
                       start=True, stop=False)
                    mm(o, ones_row[:, :], bo_row[:, :], start=False, stop=False)
                    if j == 0:
                        mm(o, pT_cs[:, 0, :], vwc[:, 0, :], start=False, stop=False)
                        mm(o, pT_cs[0:SELECT_K, 1, :], vwc[0:SELECT_K, 1, :], start=False, stop=False)
                    last = mm(o, pT_win[:, j, :], vww[:, j, :], start=False, stop=True)
                last.then_inc(out_ready, 1)

            def body(b, first=False, last=False):
                for j in range(TB):
                    n = TB * b + j
                    if not (last and j == TB - 1):
                        scores(n + 1, (j + 1) % TB, b + (j + 1) // TB, first)
                    if j == 0:
                        project_windows(b)
                    if j == 1:
                        if first:
                            pe.wait_ge(y_stored, 16)
                            nc.tensor.transpose(f_bank[:, 0:TILES], rank32[:, :],
                                                ident[0:TILES, 0:TILES]).then_inc(rankT_ready, 1)
                        project_selected(b)
                        attention_scores(b, first)
                    if j == 2:
                        values_out(b)
                        if not first:
                            experts_out(b - 1)
                    if j == 3:
                        attention_out(b, first)
                    if not (first and n < 2):
                        if j == 2 and not first:
                            pe.wait_ge(c_out, b)
                        expert_weights(n - 2, (j + 2) % TB, first)

            pe.wait_ge(w_att, 16 * W_ATT)
            transpose_rows(0)
            for b in range(B):
                if b + 1 < B:
                    transpose_rows(b + 1)
                logits(b)
                if b == 2:
                    pe.wait_ge(prep_dve, 2)
                    scores(0, 0, 0, True)
            pe.wait_ge(z_out, B)
            gate_columns(B - 1).then_inc(zg_full, 1)
            pe.wait_ge(w_late, 16 * W_LATE)
            body(0, first=True)
            with pe.Fori(1, B - 1) as b:
                body(b)
            body(B - 1, last=True)
            expert_weights(TILES - 2, 2)
            expert_weights(TILES - 1, 3)
            experts_out(B - 1)


_INS = ["L0_attn_hidden_states", "L0_attn_Wq", "L0_attn_bq", "L0_attn_Wk", "L0_attn_bk", "L0_attn_Wv",
        "L0_attn_bv", "L0_attn_Wo", "L0_attn_bo", "L0_attn_Wg", "L0_attn_bg", "L0_attn_Wc", "L0_attn_bc",
        "L0_attn_Ws", "L0_attn_bs", "L0_ffn_Wq", "L0_ffn_keys", "L0_ffn_W_down", "L0_ffn_W_up"]


def kernel(**inputs):
    import numpy as np
    import concourse.bacc as bacc
    from concourse.bass_utils import run_bass_kernel_spmd

    nc = bacc.Bacc("TRN2", target_bir_lowering=False, num_devices=1)
    arrays, args = {}, []
    for name in _INS:
        a = np.ascontiguousarray(inputs[name])
        arrays[f"in_{name}"] = a
        args.append(nc.dram_tensor(f"in_{name}", a.shape, mybir.dt.from_np(a.dtype), kind="ExternalInput").ap())
    shape = inputs["L0_attn_hidden_states"].shape
    args.append(nc.dram_tensor("out_0", shape, F32, kind="ExternalOutput").ap())
    program(nc, *args)
    r = run_bass_kernel_spmd(nc, [arrays], core_ids=[0])
    return r.results[0]["out_0"]
```

```python
from contextlib import ExitStack

import concourse.bass as bass
from concourse import mybir
from concourse.alu_op_type import AluOpType as ALU

F32 = mybir.dt.float32
ACT = mybir.ActivationFunctionType
AX_X = mybir.AxisListType.X

P = 128
RATIO = 4
SELECT_K = 64
WINDOW = 32
STEP_W = WINDOW // 2
N_HEADS = 16
COMP, SEL, WIN = range(3)
HEADS = 8
KEYS = 32
DKEY = 64
TOPK = 16
VECS = 2 * HEADS
ROW_LEN = [TOPK // (i + 1) for i in range(TOPK)]
CANDS = sum(ROW_LEN)
EARLY_LEN = [8 // (i + 1) for i in range(8)]
EARLY = sum(EARLY_LEN)


def runs_of(row_len):
    runs, at = [], 0
    for i, n in enumerate(row_len):
        if runs and runs[-1][2] == n:
            runs[-1][1] += 1
        else:
            runs.append([i, 1, n, at])
        at += n
    return runs


RUNS = runs_of(ROW_LEN)
TAKEN = -1e30
NO_SCORE = -3.3e38
HALF_V = VECS // 2
HALF_H = HEADS // 2


def program(nc, x, wq, bq, wk, bk, wv, bv, wo, bo, wg, bg, wc, bc, ws, bs,
            ffn_wq, ffn_keys, ffn_down, ffn_up, out):
    B, L, D = x.shape
    assert D == P and L % P == 0 and B % 2 == 0
    TB = L // P
    TILES = B * TB
    BLOCKS = L // RATIO
    WPT = P // WINDOW
    WKEYS = STEP_W * (WPT - 1) + WINDOW
    WTOK = STEP_W * WPT * (TB - 1) + WKEYS
    CS = BLOCKS + SELECT_K
    LAST = 2
    SCALE = float((D // N_HEADS) ** -0.5)
    HK = HEADS * KEYS
    assert TB == 4 and BLOCKS == P and TB * WKEYS + CS <= 512 and 2 * HK <= 512

    ctx = ExitStack()
    with ctx:
        def sb(name, shape, dt=F32):
            return ctx.enter_context(nc.sbuf_tensor(name, shape, dt))

        def bank(name):
            return ctx.enter_context(nc.psum_tensor(name, [P, 512], F32))

        def sem(name):
            return ctx.enter_context(nc.semaphore(name))

        sim_bank = [bank(f"sim{i}") for i in range(2)]
        scratch = [bank(f"scratch{i}") for i in range(2)]
        s_bank = bank("s_bank")
        out_bank = bank("out_bank")
        c_bank = bank("c_bank")
        f_bank = bank("f_bank")
        side_bank = [c_bank, out_bank]
        last_c, last_f = sim_bank
        z_bank = s_bank

        ident = sb("ident", [P, P])
        ones_row = sb("ones_row", [1, TB * P])
        rank_row = sb("rank_row", [P, SELECT_K])
        neg_half = sb("neg_half", [P, TILES])
        win_mask = sb("win_mask", [P, TB, WKEYS])
        wq_sb, wk_sb, wv_sb = (sb(n, [P, D]) for n in ("wq_sb", "wk_sb", "wv_sb"))
        wc_sb = sb("wc_sb", [P, RATIO, D])
        wo_sb = sb("wo_sb", [P, 3, D])
        bq_sb, bqs_sb, bk_sb, bv_sb, bc_sb = (sb(n, [P, 1]) for n in ("bq_sb", "bqs_sb", "bk_sb", "bv_sb", "bc_sb"))
        bz_sb = sb("bz_sb", [4 * B, 1])
        fwq_sb = sb("fwq_sb", [P, HEADS, D])
        keys_sb = sb("keys_sb", [P, 2, P])
        keysT = sb("keysT", [P, HEADS, 2, KEYS])
        sim_w = sb("sim_w", [P, VECS * KEYS])
        down_sb = sb("down_sb", [CANDS, D])
        downT = sb("downT", [P, CANDS])
        zw_sb = sb("zw_sb", [P, 4])
        zw_rows = sb("zw_rows", [P, B, 4, B])
        up_sb = sb("up_sb", [CANDS, D])

        x_sb = sb("x_sb", [P, TILES, D])
        xn_all = sb("xn_all", [P, TILES, D])
        xT_all = sb("xT_all", [P, TILES * P])
        xTc = sb("xTc", [P, TB, P])
        st1 = sb("st1", [P, TILES, 6])
        mv1 = sb("mv1", [P, TILES, 2])
        var1, rstd1, prod1, nmr1 = (sb(n, [P, TILES]) for n in ("var1", "rstd1", "prod1", "nmr1"))
        geluT = sb("geluT", [CANDS, TILES * P])
        z_sb = sb("z_sb", [4 * B, L])
        gexp = sb("gexp", [P, 3, TB, B])
        gsig = sb("gsig", [P, 3, TILES])
        gsum = sb("gsum", [P, TILES])
        gates = sb("gates", [P, 3, TB, B])

        sel_a = sb("sel_a", [B, L])
        sel_b = sb("sel_b", [B, L])
        sel_m = sb("sel_m", [B, 8])
        sel_mask = sb("sel_mask", [B, L])
        sel_cnt = sb("sel_cnt", [B, L])
        sel_rank = sb("sel_rank", [B, L])
        zero_row = sb("zero_row", [B, L])
        rankT = sb("rankT", [P, TB, B])
        pick = sb("pick", [P, TB, SELECT_K])

        qw = sb("qw", [P, L])
        kw, vw = (sb(n, [P, WTOK]) for n in ("kw", "vw"))
        xsel = sb("xsel", [SELECT_K, D])
        csT = sb("csT", [P, CS])
        qcs, kcs, vcs = (sb(n, [P, CS]) for n in ("qcs", "kcs", "vcs"))
        vww = sb("vww", [WKEYS + 1, TB, D])
        vwc = sb("vwc", [P, 2, D])
        nmax = sb("nmax", [P, 6])
        rsum = sb("rsum", [P, 6])
        rinv = sb("rinv", [P, 6])
        rgate = sb("rgate", [P, 6])
        p_win = sb("p_win", [P, TB, WKEYS])
        p_cs = sb("p_cs", [P, CS])
        pT_win = sb("pT_win", [WKEYS + 1, TB, P])
        pT_cs = sb("pT_cs", [P, 2, P])
        spare = sb("spare", [P, 2, TB, D])
        sum2, nmean2, sq2, var2, rstd2, nmr2 = (
            sb(n, [P, TB]) for n in ("sum2", "nmean2", "sq2", "var2", "rstd2", "nmr2"))
        s_norm = sb("s_norm", [P, TB, D])

        top = [sb(f"top{i}", [P, VECS, TOPK]) for i in range(2)]
        rest = sb("rest", [P, VECS, KEYS])
        shifted = sb("shifted", [P, VECS, TOPK])
        cand = [sb(f"cand{i}", [P, HEADS, CANDS]) for i in range(2)]
        early = [sb(f"early{i}", [P, HEADS, EARLY]) for i in range(2)]
        crest = sb("crest", [P, HEADS, CANDS])
        left = [sb(f"left{i}", [P, HEADS, CANDS]) for i in range(2)]
        best = [sb(f"best{i}", [P, HEADS, TOPK]) for i in range(2)]
        e_best = sb("e_best", [P, HEADS, TOPK])
        e_all = [sb(f"e_all{i}", [P, HEADS, CANDS]) for i in range(2)]
        e_left = [sb(f"e_left{i}", [P, HEADS, CANDS]) for i in range(2)]
        den = [sb(f"den{i}", [P, HEADS]) for i in range(2)]
        rden = [sb(f"rden{i}", [P, HEADS]) for i in range(2)]
        prob = sb("prob", [P, HEADS, CANDS])
        wgt = [sb(f"wgt{i}", [P, HEADS, CANDS]) for i in range(2)]
        wsum = sb("wsum", [P, LAST, CANDS])
        c_sb = sb("c_sb", [CANDS, L])
        actT = sb("actT", [CANDS, L])
        tanh_f = sb("tanh_f", [P, TB, D])
        tanh1_f = sb("tanh1_f", [P, TB, D])
        half_f = sb("half_f", [P, TB, D])
        y1 = sb("y1", [P, TB, D])
        y3 = sb("y3", [P, TB, D])
        y_sb = sb("y_sb", [P, TB, D])

        x_in = [sem(f"x_in{i}") for i in range(4)]
        keys_in, fwq_in, zw_in, down_in, w_late = (
            sem(n) for n in ("keys_in", "fwq_in", "zw_in", "down_in", "w_late"))
        FWQ_DMAS, ZW_DMAS, DOWN_DMAS, LATE_DMAS = 2, 2 + 4, len(RUNS), 9 + TB + 1 + len(RUNS)
        bqs_done = sem("bqs_done")
        consts = sem("consts")
        keysT_ready, keysT_out, fold_ready, sim_w_done, downT_ready, downT_out = (
            sem(n) for n in ("keysT_ready", "keysT_out", "fold_ready", "sim_w_done", "downT_ready", "downT_out"))
        stats1, mean1, norm1_ready, xn_done = (
            sem("stats1"), sem("mean1"), sem("norm1_ready"), [sem("xn_done_even"), sem("xn_done_odd")])
        pool_step = sem("pool_step")
        xt_full, xt_out, side_full, side_out = (sem(n) for n in ("xt_full", "xt_out", "side_full", "side_out"))
        zw_done, z_ready, z_done, gate_ready = (sem(n) for n in ("zw_done", "z_ready", "z_done", "gate_ready"))
        unit_full, unit_out = sem("unit_full"), sem("unit_out")
        tile_in = [sem(f"tile_in{j}") for j in range(TB)]
        sim_ready, sim_top8, sim_used, top_done = sem("sim_ready"), sem("sim_top8"), sem("sim_used"), sem("top_done")
        shift_done, early_ready, cand_ready = sem("shift_done"), sem("early_ready"), sem("cand_ready")
        best8, best8_out, best_done, left_done = sem("best8"), sem("best8_out"), sem("best_done"), sem("left_done")
        exp_done, den_done, rden_done = sem("exp_done"), sem("den_done"), sem("rden_done")
        exp_last = sem("exp_last")
        prob_done, wgt_done, head_sum, c_ready, c_out = (
            sem(n) for n in ("prob_done", "wgt_done", "head_sum", "c_ready", "c_out"))
        act_done, f_ready, tanh_done, f_out = sem("act_done"), sem("f_ready"), sem("tanh_done"), sem("f_out")
        sel_step, rank_out, rankT_ready, rankT_out, pick_done = (
            sem(n) for n in ("sel_step", "rank_out", "rankT_ready", "rankT_out", "pick_done"))
        gate_exp, gate_step = sem("gate_exp"), sem("gate_step")
        s_ready, max_done, p_exp, rinv_done, rgate_done, p_scaled = (
            sem(n) for n in ("s_ready", "max_done", "p_exp", "rinv_done", "rgate_done", "p_scaled"))
        out_ready, sums2, mean2, squares2, norm2_step, norm2_ready, s_done = (
            sem(n) for n in ("out_ready", "sums2", "mean2", "squares2", "norm2_step", "norm2_ready", "s_done"))
        y_step, y_free, y_done, y_stored = sem("y_step"), sem("y_free"), sem("y_done"), sem("y_stored")

        NORM_GROUPS = [(0, 1), (1, 2), (2, 4), (4, 6), (6, B)]
        POOL_NORMS = [1, 2, 4]
        ACT_NORMS = [3, 5, 6, 7]
        X_PARTS = [(0, 1), (1, 2), (2, 4), (4, B)]
        M_UNITS = 12
        (U_QW, U_KW, U_VW, U_COMP, U_SEL, U_SELT, U_QK, U_V,
         U_VWW, U_VWC, U_PTW, U_PTC) = range(M_UNITS)

        def m_unit(b, k):
            return M_UNITS * b + k

        x_v = x.rearrange("b (t p) d -> p (b t) d", p=P)
        out_v = out.rearrange("b (t p) d -> p (b t) d", p=P)

        CONSTS = 5 + WPT

        passed = {e: sem(f"passed_{i}") for i, e in enumerate(nc.engines)}

        def wait_reg(eng, signal, value):
            eng.wait_ge(signal, value)
            if not isinstance(value, int):
                eng.sem_inc(passed[eng.engine], 1)

        def load_experts(eng, dst, src, signal):
            for i0, rows, length, at in RUNS:
                part = src[i0 * TOPK:(i0 + rows) * TOPK, :].rearrange("(i j) d -> i j d", j=TOPK)[:, 0:length, :]
                eng.dma_start(dst[at:at + rows * length, :], part).then_inc(signal, 16)

        block = ctx.enter_context(nc.Block())

        @block.sync
        def _(sp):
            for i, (b0, b1) in enumerate(X_PARTS):
                sp.dma_start(x_sb[:, TB * b0:TB * b1, :], x_v[:, TB * b0:TB * b1, :]).then_inc(x_in[i], 16)
            sp.dma_start(zw_sb[:, 0:1], ws[:, :]).then_inc(zw_in, 16)
            sp.dma_start(zw_sb[:, 1:4], wg[:, :]).then_inc(zw_in, 16)
            for k, src in enumerate([bs[0:1], bg[0:1], bg[1:2], bg[2:3]]):
                sp.dma_start(bz_sb[k * B:(k + 1) * B, :],
                             src.rearrange("(a n) -> a n", a=1).to_broadcast([B, 1])).then_inc(zw_in, 16)
            load_experts(sp, down_sb, ffn_down, down_in)
            for dst, src in ((wq_sb, wq), (wk_sb, wk), (wv_sb, wv)):
                sp.dma_start(dst[:, :], src[:, :]).then_inc(w_late, 16)
            for dst, src in ((bq_sb, bq), (bk_sb, bk), (bv_sb, bv), (bc_sb, bc)):
                sp.dma_start(dst[:, :], src.rearrange("(n a) -> n a", a=1)).then_inc(w_late, 16)
            sp.dma_start(wc_sb[:, :, :], wc.rearrange("(r p) n -> p r n", p=P)).then_inc(w_late, 16)
            sp.dma_start(wo_sb[:, :, :], wo.rearrange("(r p) n -> p r n", p=P)).then_inc(w_late, 16)
            for j in range(TB):
                sp.dma_start(vww[WKEYS:WKEYS + 1, j, :], bo.rearrange("(a n) -> a n", a=1)).then_inc(w_late, 16)
            sp.wait_ge(consts, CONSTS)
            sp.dma_start(pT_win[WKEYS:WKEYS + 1, :, :], ones_row[:, :].rearrange("a (t p) -> a t p", t=TB)
                         ).then_inc(w_late, 16)
            load_experts(sp, up_sb, ffn_up, w_late)

            def load_tiles(b):
                for j in range(TB):
                    sp.wait_ge(sim_ready, TB * (b - 1) + j + 1)
                    sp.dma_start(xTc[:, j, :], xT_all[:, bass.ds((TB * b + j) * P, P)]).then_inc(tile_in[j], 16)

            def store_y(b):
                sp.wait_ge(y_done, b + 1)
                sp.dma_start(out_v[:, bass.ts(b, TB), :], y_sb[:, :, :]).then_inc(y_stored, 16)

            sp.sem_inc(y_free, 1)
            sp.wait_ge(xt_out, 2)
            load_tiles(1)
            sp.wait_ge(xt_out, B)
            with sp.Fori(2, B) as b:
                load_tiles(b)
                store_y(b - 2)
                sp.wait_ge(y_stored, 16 * (b - 1))
                sp.sem_inc(y_free, 1)
            store_y(B - 2)
            sp.wait_ge(y_stored, 16 * (B - 1))
            sp.sem_inc(y_free, 1)
            sp.wait_ge(y_done, B)
            sp.dma_start(out_v[:, TILES - TB:TILES - LAST, :], y_sb[:, 0:TB - LAST, :]).then_inc(y_stored, 16)
            sp.wait_ge(y_done, B + 1)
            sp.dma_start(out_v[:, TILES - LAST:TILES, :], y_sb[:, TB - LAST:TB, :]).then_inc(y_stored, 16)
            sp.wait_ge(y_stored, 16 * (B + 1))

        @block.gpsimd
        def _(pool):
            steps = [0]

            def step(ins):
                steps[0] += 1
                ins.then_inc(consts, 1)
                pool.wait_ge(consts, steps[0])

            nc.gpsimd.memset(zw_rows[:, :, :, :], 0.0)
            step(nc.gpsimd.memset(keysT[:, :, :, :], 0.0))
            step(nc.gpsimd.memset(ident[:, :], 0.0))
            step(nc.gpsimd.affine_select(out=ident[:, :], in_=ident[:, :], compare_op=ALU.not_equal, fill=1.0,
                                         base=0, pattern=[[-1, P]], channel_multiplier=1))
            nc.gpsimd.memset(neg_half[:, :], -0.5)
            nc.gpsimd.memset(ones_row[:, :], 1.0)
            nc.gpsimd.memset(zero_row[:, :], 0.0)
            nc.gpsimd.memset(rsum[:, :], 1.0)
            nc.gpsimd.memset(pT_cs[:, :, :], 0.0)
            step(nc.gpsimd.memset(win_mask[:, :, :], TAKEN))
            for w in range(WPT):
                step(nc.gpsimd.memset(win_mask[w * WINDOW:(w + 1) * WINDOW, :, w * STEP_W:w * STEP_W + WINDOW], 0.0))
            step(nc.gpsimd.iota(rank_row[:, :], pattern=[[1, SELECT_K]], base=1, channel_multiplier=0,
                                allow_small_or_imprecise_dtypes=True))

            for g, (b0, b1) in enumerate(NORM_GROUPS):
                pool.wait_ge(mean1, b1)
                t = slice(TB * b0, TB * b1)
                nc.gpsimd.tensor_scalar(var1[:, t], mv1[:, t, 1], 1e-5, None, ALU.add).then_inc(pool_step, 1)
                pool.wait_ge(pool_step, 3 * g + 1)
                nc.gpsimd.tensor_tensor(rstd1[:, t], var1[:, t], neg_half[:, t], ALU.pow).then_inc(pool_step, 1)
                pool.wait_ge(pool_step, 3 * g + 2)
                nc.gpsimd.tensor_tensor(prod1[:, t], mv1[:, t, 0], rstd1[:, t], ALU.mult).then_inc(pool_step, 1)
                pool.wait_ge(pool_step, 3 * g + 3)
                nc.gpsimd.tensor_scalar(nmr1[:, t], prod1[:, t], -1.0, None, ALU.mult).then_inc(norm1_ready, 1)
                pool.wait_ge(norm1_ready, g + 1)
                for b in range(b0, b1):
                    if b in POOL_NORMS:
                        for t in range(TB * b, TB * b + TB):
                            last = nc.gpsimd.tensor_scalar(xn_all[:, t, :], x_sb[:, t, :], rstd1[:, t:t + 1],
                                                           nmr1[:, t:t + 1], ALU.mult, ALU.add)
                        last.then_inc(xn_done[b % 2], 1)

            def build_cands(n, j, first):
                d = j % 2
                pool.wait_ge(top_done, 2 * n + 2)
                if not (first and n < 1):
                    pool.wait_ge(cand_ready, n)
                nc.gpsimd.tensor_tensor(shifted[:, :, :], top[d][:, :, :],
                                        top[d][:, :, 0:1].to_broadcast([P, VECS, TOPK]),
                                        ALU.subtract).then_inc(shift_done, 1)
                pool.wait_ge(shift_done, n + 1)
                if not (first and n < 2):
                    pool.wait_ge(left_done, 2 * n - 2)
                    pool.wait_ge(exp_done, n - 1)
                for dst, runs, done in ((early[d], runs_of(EARLY_LEN), early_ready), (cand[d], RUNS, cand_ready)):
                    for i0, rows, length, at in runs:
                        o = dst[:, :, at:at + rows * length].rearrange("p h (i j) -> p h i j", i=rows)
                        a = shifted[:, 0:HEADS, i0:i0 + rows].unsqueeze(3).to_broadcast([P, HEADS, rows, length])
                        c = shifted[:, HEADS:VECS, 0:length].unsqueeze(2).to_broadcast([P, HEADS, rows, length])
                        last = nc.gpsimd.tensor_tensor(o, a, c, ALU.add)
                    last.then_inc(done, 1)

            def weigh(n, j, first=False):
                d = j % 2
                pool.wait_ge(exp_done, n + 1)
                if not (first and n < 1):
                    pool.wait_ge(wgt_done, n)
                nc.gpsimd.tensor_tensor(prob[:, :, :], e_all[d][:, :, :], e_left[d][:, :, :],
                                        ALU.subtract).then_inc(prob_done, 1)
                pool.wait_ge(prob_done, n + 1)
                pool.wait_ge(rden_done, n + 1)
                if not (first and n < 2):
                    pool.wait_ge(c_ready, n - 1)
                nc.gpsimd.tensor_tensor(wgt[d][:, :, :], prob[:, :, :],
                                        rden[d][:, :].unsqueeze(2).to_broadcast([P, HEADS, CANDS]),
                                        ALU.mult).then_inc(wgt_done, 1)

            def gelu_times_weights(b, t1=TB):
                pool.wait_ge(c_out, b + 1)
                nc.gpsimd.tensor_tensor(actT[:, 0:t1 * P], geluT[:, bass.ds(b * L, t1 * P)], c_sb[:, 0:t1 * P],
                                        ALU.mult).then_inc(act_done, 1)

            def scale_probs(b):
                pool.wait_ge(rinv_done, b + 1)
                nc.gpsimd.tensor_tensor(rgate[:, 0:TB], rinv[:, 0:TB], gates[:, WIN, :, bass.ds(b, 1)].rearrange("p t a -> p (t a)"), ALU.mult)
                nc.gpsimd.tensor_tensor(rgate[:, TB:TB + 2], rinv[:, TB:TB + 2],
                                        gates[:, COMP:SEL + 1, 0, bass.ds(b, 1)].rearrange("p g a -> p (g a)"),
                                        ALU.mult).then_inc(rgate_done, 1)
                pool.wait_ge(rgate_done, b + 1)
                nc.gpsimd.tensor_tensor(p_win[:, :, :], p_win[:, :, :],
                                        rgate[:, 0:TB].unsqueeze(2).to_broadcast([P, TB, WKEYS]), ALU.mult)
                nc.gpsimd.tensor_tensor(p_cs[:, 0:BLOCKS], p_cs[:, 0:BLOCKS],
                                        rgate[:, TB:TB + 1].to_broadcast([P, BLOCKS]), ALU.mult)
                nc.gpsimd.tensor_tensor(p_cs[0:SELECT_K, BLOCKS:CS], p_cs[0:SELECT_K, BLOCKS:CS],
                                        rgate[0:SELECT_K, TB + 1:TB + 2].to_broadcast([SELECT_K, SELECT_K]),
                                        ALU.mult).then_inc(p_scaled, 1)

            def norm2(b):
                wait_reg(pool, squares2, b + 1)
                nc.gpsimd.tensor_scalar(var2[:, :], sq2[:, :], 1.0 / D, 4e-6, ALU.mult, ALU.add).then_inc(norm2_step, 1)
                pool.wait_ge(norm2_step, 2 * b + 1)
                nc.gpsimd.tensor_tensor(rstd2[:, :], var2[:, :], neg_half[:, 0:TB], ALU.pow).then_inc(norm2_step, 1)
                pool.wait_ge(norm2_step, 2 * b + 2)
                nc.gpsimd.tensor_tensor(nmr2[:, :], nmean2[:, :], rstd2[:, :], ALU.mult).then_inc(norm2_ready, 1)

            def finish_rows(b, t1=TB):
                t = slice(0, t1)
                pool.wait_ge(f_out, b + 1)
                nc.gpsimd.tensor_tensor(y1[:, t, :], tanh1_f[:, t, :], half_f[:, t, :], ALU.mult).then_inc(y_step, 1)
                pool.wait_ge(y_step, 2 * b + 1)
                pool.wait_ge(s_done, b + 1)
                nc.gpsimd.tensor_tensor(y3[:, t, :], y1[:, t, :], s_norm[:, t, :], ALU.mult).then_inc(y_step, 1)
                pool.wait_ge(y_step, 2 * b + 2)
                pool.wait_ge(y_free, b + 1)
                nc.gpsimd.tensor_tensor(y_sb[:, t, :], y3[:, t, :], x_sb[:, bass.ds(b * TB, t1), :],
                                        ALU.add).then_inc(y_done, 1)

            def body(b, first=False):
                for j in range(TB):
                    n = TB * b + j
                    if j == TB - 1 and not first:
                        scale_probs(b)
                    if not (first and n < 2):
                        weigh(n - 2, j, first)
                    if j == 2 and not first:
                        gelu_times_weights(b - 1)
                    build_cands(n, j, first)
                    if j == 0 and not first:
                        norm2(b - 1)
                    if j == TB - 1 and not first:
                        finish_rows(b - 1)
                    if j == TB - 1 and first:
                        scale_probs(b)

            body(0, first=True)
            with pool.Fori(1, B) as b:
                body(b)
            weigh(TILES - 2, 0)
            norm2(B - 1)
            gelu_times_weights(B - 1, TB - LAST)
            finish_rows(B - 1, TB - LAST)

        @block.scalar
        def _(act):
            act.dma_start(keys_sb[:, :, :], ffn_keys.rearrange("(t h) k s c -> (h k) t (s c)", t=2)).then_inc(keys_in, 16)
            for half in range(2):
                act.dma_start(fwq_sb[half * DKEY:(half + 1) * DKEY, :, :],
                              ffn_wq[bass.ts(half, HEADS * DKEY), :].rearrange("(h c) d -> c h d", h=HEADS)
                              ).then_inc(fwq_in, 16)

            def norm_rows(b):
                act.wait_ge(norm1_ready, 1 + [b0 <= b < b1 for b0, b1 in NORM_GROUPS].index(True))
                for t in range(TB * b, TB * b + TB):
                    last = nc.scalar.activation(xn_all[:, t, :], x_sb[:, t, :], ACT.Identity,
                                                bias=nmr1[:, t:t + 1], scale=rstd1[:, t:t + 1])
                last.then_inc(xn_done[b % 2], 1)

            for b in range(B):
                act.wait_ge(xt_full, b + 1)
                nc.scalar.activation(xT_all[:, bass.ts(b, L)], scratch[b % 2][:, :], ACT.Copy).then_inc(xt_out, 1)
                if b == 0:
                    act.wait_ge(consts, 1)
                    act.wait_ge(zw_in, 16 * ZW_DMAS)
                    for r in range(B):
                        last = nc.scalar.activation(zw_rows[:, r, :, r], zw_sb[:, :], ACT.Copy)
                    last.then_inc(zw_done, 1)
                if b + 2 in ACT_NORMS:
                    norm_rows(b + 2)
            act.wait_ge(z_ready, 1)
            nc.scalar.activation(z_sb[:, :], z_bank[0:4 * B, :], ACT.Identity, bias=bz_sb[:, 0:1]).then_inc(z_done, 1)
            act.wait_ge(downT_ready, 1)
            nc.scalar.activation(downT[:, :], c_bank[:, 0:CANDS], ACT.Copy).then_inc(downT_out, 1)
            for b in range(B):
                act.wait_ge(side_full, b + 1)
                nc.scalar.activation(geluT[:, bass.ts(b, L)], side_bank[b % 2][0:CANDS, :],
                                     ACT.Gelu).then_inc(side_out, 1)
            act.wait_ge(w_late, 16 * LATE_DMAS)
            nc.scalar.activation(bqs_sb[:, :], bq_sb[:, :], ACT.Copy, scale=SCALE).then_inc(bqs_done, 1)
            act.wait_ge(bqs_done, 1)
            act.wait_ge(gate_ready, 1)
            nc.scalar.activation(gexp[:, :, :, :],
                                 z_bank[:, 0:4 * TILES].rearrange("p (t g b) -> p g t b", g=4, b=B)[:, 1:4, :, :],
                                 ACT.Exp, scale=-1.0).then_inc(gate_exp, 1)

            def exps(n, j, first=False, last_tile=False):
                d = j % 2
                act.wait_ge(cand_ready, n + 1)
                if not (first and n < 2):
                    act.wait_ge(wgt_done, n - 1)
                nc.scalar.activation(e_all[d][:, :, :], cand[d][:, :, :], ACT.Exp)
                act.wait_ge(left_done, 2 * n + 2)
                nc.scalar.activation(e_left[d][:, :, :], left[d][:, :, :], ACT.Exp).then_inc(exp_done, 1)
                if not (first and n < 1):
                    act.wait_ge(den_done, n)
                if not (first and n < 2):
                    act.wait_ge(rden_done, n - 1)
                if last_tile:
                    nc.scalar.activation(e_best[:, :, :], best[d][:, :, :], ACT.Exp).then_inc(exp_last, 1)
                    return
                for h in range(HEADS):
                    last = nc.scalar.activation(e_best[:, h, :], best[d][:, h, :], ACT.Exp,
                                                accum_out=den[d][:, h:h + 1])
                last.then_inc(den_done, 1)

            def unit(b, k, outs):
                act.wait_ge(unit_full, m_unit(b, k) + 1)
                for dst, cols, bias, scale in outs:
                    src = scratch[k % 2][0:dst.shape[0], cols:cols + dst.shape[1]]
                    if bias is None:
                        last = nc.scalar.activation(dst, src, ACT.Copy)
                    else:
                        last = nc.scalar.activation(dst, src, ACT.Identity, bias=bias[:, 0:1], scale=scale)
                last.then_inc(unit_out, 1)

            def moments(b):
                act.wait_ge(out_ready, b + 1)
                for j in range(TB):
                    last = nc.scalar.activation(spare[:, 0, j, :], out_bank[:, bass.ts(j, D)], ACT.Identity,
                                                accum_out=sum2[:, j:j + 1])
                last.then_inc(sums2, 1)
                act.wait_ge(sums2, b + 1)
                nc.scalar.activation(nmean2[:, :], sum2[:, :], ACT.Copy, scale=-1.0 / D).then_inc(mean2, 1)
                act.wait_ge(mean2, b + 1)
                for j in range(TB):
                    last = nc.scalar.activation(spare[:, 1, j, :], out_bank[:, bass.ts(j, D)], ACT.Square,
                                                bias=nmean2[:, j:j + 1], accum_out=sq2[:, j:j + 1])
                last.then_inc(squares2, 1)

            def norm_attention(b):
                act.wait_ge(norm2_ready, b + 1)
                for j in range(TB):
                    last = nc.scalar.activation(s_norm[:, j, :], out_bank[:, bass.ts(j, D)], ACT.Identity,
                                                bias=nmr2[:, j:j + 1], scale=rstd2[:, j:j + 1])
                last.then_inc(s_done, 1)

            def weights_out(b, t1=TB):
                act.wait_ge(c_ready, TB * b + t1)
                nc.scalar.activation(c_sb[:, 0:t1 * P], c_bank[0:CANDS, 0:t1 * P], ACT.Copy).then_inc(c_out, 1)

            def silu_parts(b, t0=0, t1=TB):
                act.wait_ge(f_ready, b + (1 if t0 == 0 else 2))
                f_v = (f_bank if t0 == 0 else last_f)[:, :].rearrange("p (t d) -> p t d", t=TB)[:, t0:t1, :]
                nc.scalar.activation(tanh_f[:, t0:t1, :], f_v, ACT.Tanh, scale=0.5).then_inc(tanh_done, 1)
                half = nc.scalar.activation(half_f[:, t0:t1, :], f_v, ACT.Copy, scale=0.5)
                if t0 > 0:
                    half.then_inc(f_out, 1)
                    return
                act.wait_ge(tanh_done, b + 1)
                nc.scalar.activation(tanh1_f[:, t0:t1, :], tanh_f[:, t0:t1, :], ACT.Identity,
                                     bias=1.0).then_inc(f_out, 1)

            def body(b, first=False):
                for j in range(TB):
                    n = TB * b + j
                    if first and j == 1:
                        exps(0, 0, True)
                    elif not first:
                        exps(n - 2, j)
                    if j == 0 and not first:
                        moments(b - 1)
                    if j == 0:
                        act.wait_ge(unit_full, m_unit(b, U_QW) + 1)
                        overlap = bass.AP(scratch[U_QW % 2], 0, [[512, P], [STEP_W, L // WINDOW], [1, WINDOW]])
                        nc.scalar.activation(qw[:, :].rearrange("p (w t) -> p w t", t=WINDOW), overlap, ACT.Identity,
                                             bias=bqs_sb[:, 0:1], scale=SCALE).then_inc(unit_out, 1)
                        unit(b, U_KW, [(kw[:, :], 0, bk_sb, 1.0)])
                        unit(b, U_VW, [(vw[:, :], 0, bv_sb, 1.0)])
                        unit(b, U_COMP, [(csT[:, 0:BLOCKS], 0, bc_sb, 1.0)])
                    if j == 1:
                        if first:
                            act.wait_ge(rankT_ready, 1)
                            nc.scalar.activation(rankT[:, :, :], f_bank[:, 0:TILES].rearrange("p (t b) -> p t b", b=B),
                                                 ACT.Copy).then_inc(rankT_out, 1)
                        else:
                            norm_attention(b - 1)
                        unit(b, U_SEL, [(xsel[:, :], 0, None, 1.0)])
                        unit(b, U_SELT, [(csT[:, BLOCKS:CS], 0, None, 1.0)])
                        unit(b, U_QK, [(qcs[:, :], 0, bqs_sb, SCALE), (kcs[:, :], CS, bk_sb, 1.0)])
                        unit(b, U_V, [(vcs[:, :], 0, bv_sb, 1.0)])
                        if first:
                            exps(1, 1, True)
                    if j == 2:
                        if not first:
                            weights_out(b - 1)
                        unit(b, U_VWW, [(vww[0:WKEYS, :, :].rearrange("p t d -> p (t d)"), 0, None, 1.0)])
                        unit(b, U_VWC, [(vwc[:, :, :].rearrange("p t d -> p (t d)"), 0, None, 1.0)])
                    if j == (3 if first else 2):
                        act.wait_ge(max_done, b + 1)
                        for g in range(TB):
                            nc.scalar.activation(p_win[:, g, :], s_bank[:, bass.ts(g, WKEYS)], ACT.Exp,
                                                 bias=nmax[:, g:g + 1], accum_out=rsum[:, g:g + 1])
                        nc.scalar.activation(p_cs[:, 0:BLOCKS], s_bank[:, TB * WKEYS:TB * WKEYS + BLOCKS], ACT.Exp,
                                             bias=nmax[:, TB:TB + 1], accum_out=rsum[:, TB:TB + 1])
                        nc.scalar.activation(p_cs[0:SELECT_K, BLOCKS:CS],
                                             s_bank[0:SELECT_K, TB * WKEYS + BLOCKS:TB * WKEYS + CS], ACT.Exp,
                                             bias=nmax[0:SELECT_K, TB + 1:TB + 2],
                                             accum_out=rsum[0:SELECT_K, TB + 1:TB + 2]).then_inc(p_exp, 1)
                    if j == 3:
                        if not first:
                            silu_parts(b - 1)
                        unit(b, U_PTW, [(pT_win[0:WKEYS, :, :].rearrange("p t q -> p (t q)"), 0, None, 1.0)])
                        unit(b, U_PTC, [(pT_cs[:, 0, :], 0, None, 1.0),
                                        (pT_cs[0:SELECT_K, 1, 0:SELECT_K], P, None, 1.0)])

            body(0, first=True)
            with act.Fori(1, B) as b:
                body(b)
            exps(TILES - 2, 0)
            moments(B - 1)
            exps(TILES - 1, 1, last_tile=True)
            weights_out(B - 1, TB - LAST)
            norm_attention(B - 1)
            silu_parts(B - 1, 0, TB - LAST)
            silu_parts(B - 1, TB - LAST, TB)

        @block.vector
        def _(dve):
            def stats_of(src, st, mv, counter, before, done):
                for j in range(TB):
                    last = nc.vector.bn_stats(st[:, j, :], src(j))
                last.then_inc(counter, 1)
                wait_reg(dve, counter, before + 1)
                for j in range(TB):
                    last = nc.vector.bn_aggr(mv[:, j, :], st[:, j, :])
                last.then_inc(done, 1)

            def row_stats(b):
                t = TB * b
                stats_of(lambda j: x_sb[:, t + j, :], st1[:, t:t + TB, :], mv1[:, t:t + TB, :], stats1, b, mean1)

            dve.wait_ge(x_in[0], 16)
            row_stats(0)
            dve.wait_ge(consts, 1)
            dve.wait_ge(keysT_ready, 1)
            for half in range(2):
                c = slice(half * DKEY, (half + 1) * DKEY)
                last = nc.vector.tensor_copy(keysT[c, :, half, :], f_bank[c, 0:HK].rearrange("p (h k) -> p h k", k=KEYS))
            last.then_inc(keysT_out, 1)
            dve.wait_ge(norm1_ready, 1)
            for t in range(TB):
                last = nc.vector.tensor_scalar(xn_all[:, t, :], x_sb[:, t, :], rstd1[:, t:t + 1],
                                               nmr1[:, t:t + 1], ALU.mult, ALU.add)
            last.then_inc(xn_done[0], 1)
            for b in range(1, B):
                for i, (b0, b1) in enumerate(X_PARTS):
                    if b == b0:
                        dve.wait_ge(x_in[i], 16)
                if b == 3:
                    dve.wait_ge(fold_ready, 1)
                    nc.vector.tensor_copy(sim_w[:, :].rearrange("p (s h k) -> p h s k", s=2, h=HEADS),
                                          sim_bank[1][:, :].rearrange("p (h s k) -> p h s k", s=2, h=HEADS)
                                          ).then_inc(sim_w_done, 1)
                if b < 6:
                    row_stats(b)

            def invert_sums(n, j, first):
                d = j % 2
                wait_reg(dve, den_done, n + 1)
                if not (first and n < 2):
                    dve.wait_ge(wgt_done, n - 1)
                nc.vector.reciprocal(rden[d][:, :], den[d][:, :]).then_inc(rden_done, 1)

            def sort_scores(n, j, first=False, dens=True, midway=None):
                d = j % 2
                if first and n == 2:
                    pass
                else:
                    if not (first and n < 2):
                        dve.wait_ge(shift_done, n - 1)
                    wait_reg(dve, sim_ready, n + 1)
                    for h in range(2):
                        for v in range(h * HALF_V, (h + 1) * HALF_V):
                            last = nc.vector.max(top[d][:, v, 0:8], sim_bank[d][:, bass.ts(v, KEYS)])
                        last.then_inc(sim_top8, 1)
                for h in range(2):
                    if not (first and n < 1):
                        dve.wait_ge(top_done, 2 * n - 1 + h)
                    wait_reg(dve, sim_top8, 2 * n + 1 + h)
                    for v in range(h * HALF_V, (h + 1) * HALF_V):
                        last = nc.vector.match_replace(out=rest[:, v, :], in_to_replace=top[d][:, v, 0:8],
                                                       in_values=sim_bank[d][:, bass.ts(v, KEYS)],
                                                       imm_value=NO_SCORE)
                    last.then_inc(sim_used, 1)
                if midway is not None:
                    midway()
                for h in range(2):
                    wait_reg(dve, sim_used, 2 * n + 1 + h)
                    for v in range(h * HALF_V, (h + 1) * HALF_V):
                        last = nc.vector.max(top[d][:, v, 8:16], rest[:, v, :])
                    last.then_inc(top_done, 1)
                    if dens and h == 0:
                        invert_sums(n - 2, j, first)

            def take_best(n, j, first=False, midway=None):
                d = j % 2
                halves = [range(h * HALF_H, (h + 1) * HALF_H) for h in range(2)]
                if not (first and n < 2):
                    dve.wait_ge(den_done, n - 1)
                wait_reg(dve, early_ready, n + 1)
                for hs in halves:
                    for h in hs:
                        last = nc.vector.max(best[d][:, h, 0:8], early[d][:, h, :])
                    last.then_inc(best8, 1)
                if not (first and n < 1):
                    dve.wait_ge(left_done, 2 * n)
                wait_reg(dve, cand_ready, n + 1)
                for k, hs in enumerate(halves):
                    wait_reg(dve, best8, 2 * n + 1 + k)
                    for h in hs:
                        last = nc.vector.match_replace(out=crest[:, h, :], in_to_replace=best[d][:, h, 0:8],
                                                       in_values=cand[d][:, h, :], imm_value=TAKEN)
                    last.then_inc(best8_out, 1)
                if midway is not None:
                    midway()
                for k, hs in enumerate(halves):
                    wait_reg(dve, best8_out, 2 * n + 1 + k)
                    for h in hs:
                        last = nc.vector.max(best[d][:, h, 8:16], crest[:, h, :])
                    last.then_inc(best_done, 1)
                if not (first and n < 2):
                    dve.wait_ge(exp_done, n - 1)
                for k, hs in enumerate(halves):
                    wait_reg(dve, best_done, 2 * n + 1 + k)
                    for h in hs:
                        last = nc.vector.match_replace(out=left[d][:, h, :], in_to_replace=best[d][:, h, 8:16],
                                                       in_values=crest[:, h, :], imm_value=TAKEN)
                    last.then_inc(left_done, 1)

            def chain(n_done, ins):
                ins.then_inc(sel_step, 1)
                dve.wait_ge(sel_step, n_done)

            def select_tokens(n):
                d = n % 2
                dve.wait_ge(sim_ready, n + 1)
                dve.wait_ge(shift_done, n - 1)
                dve.wait_ge(z_done, 1)
                dve.wait_ge(consts, CONSTS)
                k = 0
                src, dst = z_sb[0:B, :], sel_a
                for r in range(SELECT_K // 8):
                    nc.vector.max(sel_m[:, :], src[:, :]).then_inc(sel_step, 1)
                    nc.vector.max(top[d][:, 2 * r, 0:8], sim_bank[d][:, bass.ts(2 * r, KEYS)])
                    dve.wait_ge(sel_step, k + 1)
                    nc.vector.match_replace(out=dst[:, :], in_to_replace=sel_m[:, :],
                                            in_values=src[:, :], imm_value=NO_SCORE).then_inc(sel_step, 1)
                    last = nc.vector.max(top[d][:, 2 * r + 1, 0:8], sim_bank[d][:, bass.ts(2 * r + 1, KEYS)])
                    if 2 * (r + 1) % HALF_V == 0:
                        last.then_inc(sim_top8, 1)
                    k += 2
                    dve.wait_ge(sel_step, k)
                    src, dst = dst, (sel_b if dst is sel_a else sel_a)
                k += 1
                chain(k, nc.vector.tensor_scalar(sel_mask[:, :], src[:, :], NO_SCORE, None, ALU.is_equal))
                k += 1
                chain(k, nc.vector.tensor_tensor_scan(sel_cnt[:, :], sel_mask[:, :], zero_row[0:B, :], 0.0,
                                                      ALU.add, ALU.add))
                nc.vector.tensor_tensor(sel_rank[:, :], sel_cnt[:, :], sel_mask[:, :], ALU.mult).then_inc(rank_out, 1)

            def normalise_gates():
                dve.wait_ge(gate_exp, 1)
                k = [0]

                def link(ins):
                    k[0] += 1
                    ins.then_inc(gate_step, 1)
                    dve.wait_ge(gate_step, k[0])

                link(nc.vector.tensor_scalar(gexp[:, :, :, :], gexp[:, :, :, :], 1.0, None, ALU.add))
                link(nc.vector.reciprocal(gsig[:, :, :], gexp[:, :, :, :].rearrange("p g t b -> p g (t b)")))
                link(nc.vector.tensor_reduce(gsum[:, :], gsig[:, :, :].rearrange("p g n -> p n g"), AX_X, ALU.add))
                link(nc.vector.tensor_scalar(gsum[:, :], gsum[:, :], 1e-6, None, ALU.add))
                link(nc.vector.reciprocal(gsum[:, :], gsum[:, :]))
                link(nc.vector.tensor_tensor(gates[:, :, :, :].rearrange("p g t b -> p g (t b)"), gsig[:, :, :],
                                             gsum[:, :].unsqueeze(1).to_broadcast([P, 3, TILES]), ALU.mult))

            def pick_matrix(b):
                nc.vector.tensor_tensor(pick[:, :, :], rank_row[:, :].unsqueeze(1).to_broadcast([P, TB, SELECT_K]),
                                        rankT[:, :, bass.ds(b, 1)].to_broadcast([P, TB, SELECT_K]),
                                        ALU.is_equal).then_inc(pick_done, 1)

            def inverse_row_sums(b):
                dve.wait_ge(p_exp, b + 1)
                nc.vector.reciprocal(rinv[:, :], rsum[:, :]).then_inc(rinv_done, 1)

            def first_pick():
                dve.wait_ge(rankT_out, 1)
                pick_matrix(0)

            def maxima(b):
                dve.wait_ge(s_ready, b + 1)
                nc.vector.tensor_reduce(nmax[:, 0:TB], s_bank[:, 0:TB * WKEYS].rearrange("p (g k) -> p g k", g=TB),
                                        AX_X, ALU.max, negate=True)
                nc.vector.tensor_reduce(nmax[:, TB:TB + 1], s_bank[:, TB * WKEYS:TB * WKEYS + BLOCKS], AX_X, ALU.max,
                                        negate=True)
                nc.vector.tensor_reduce(nmax[0:SELECT_K, TB + 1:TB + 2],
                                        s_bank[0:SELECT_K, TB * WKEYS + BLOCKS:TB * WKEYS + CS], AX_X, ALU.max,
                                        negate=True).then_inc(max_done, 1)

            def body(b, first=False):
                for j in range(TB):
                    n = TB * b + j
                    sort_scores(n, j, first, not (first and j < 2), first_pick if first and j == 2 else None)
                    if first and j == 0:
                        row_stats(6)
                        row_stats(7)
                    if j == (3 if first else 2):
                        maxima(b)
                    if not (first and n < 1):
                        take_best(n - 1, j - 1, first, (lambda: inverse_row_sums(0)) if first and j == 3 else None)
                    if first and j == 2:
                        normalise_gates()
                    if j == 0 and not first:
                        pick_matrix(b)
                    if first and j == 1:
                        select_tokens(2)
                    if j == 2 and not first:
                        inverse_row_sums(b)

            body(0, first=True)
            with dve.Fori(1, B) as b:
                body(b)
            take_best(TILES - 1, 1, midway=lambda: invert_sums(TILES - 2, 0, False))

            n, d, b = TILES - 1, (TILES - 1) % 2, B - 1
            t, cols = slice(TB - LAST, TB), slice(0, LAST * P)
            dve.wait_ge(wgt_done, n)
            nc.vector.tensor_reduce(wsum[:, 0, :], wgt[1 - d][:, :, :].rearrange("p h c -> p c h"), AX_X,
                                    ALU.add).then_inc(head_sum, 1)
            dve.wait_ge(exp_last, 1)
            nc.vector.tensor_reduce(den[d][:, :], e_best[:, :, :], AX_X, ALU.add).then_inc(den_done, 1)
            invert_sums(n, 1, False)
            dve.wait_ge(exp_done, n + 1)
            nc.vector.tensor_tensor(prob[:, :, :], e_all[d][:, :, :], e_left[d][:, :, :],
                                    ALU.subtract).then_inc(prob_done, 1)
            dve.wait_ge(prob_done, n + 1)
            dve.wait_ge(rden_done, n + 1)
            dve.wait_ge(c_ready, n - 1)
            nc.vector.tensor_tensor(wgt[d][:, :, :], prob[:, :, :],
                                    rden[d][:, :].unsqueeze(2).to_broadcast([P, HEADS, CANDS]),
                                    ALU.mult).then_inc(wgt_done, 1)
            dve.wait_ge(wgt_done, n + 1)
            nc.vector.tensor_reduce(wsum[:, 1, :], wgt[d][:, :, :].rearrange("p h c -> p c h"), AX_X,
                                    ALU.add).then_inc(head_sum, 1)
            dve.wait_ge(act_done, B)
            dve.wait_ge(c_ready, n + 1)
            nc.vector.tensor_tensor(actT[:, (TB - LAST) * P:L], geluT[:, (TILES - LAST) * P:TILES * P],
                                    last_c[0:CANDS, cols], ALU.mult).then_inc(act_done, 1)
            dve.wait_ge(y_step, 2 * B)
            dve.wait_ge(f_out, B + 1)
            nc.vector.scalar_tensor_tensor(y1[:, t, :], tanh_f[:, t, :], 1.0, half_f[:, t, :],
                                           ALU.add, ALU.mult).then_inc(y_step, 1)
            dve.wait_ge(y_step, 2 * B + 1)
            dve.wait_ge(s_done, b + 1)
            nc.vector.tensor_tensor(y3[:, t, :], y1[:, t, :], s_norm[:, t, :], ALU.mult).then_inc(y_step, 1)
            dve.wait_ge(y_step, 2 * B + 2)
            dve.wait_ge(y_done, B)
            nc.vector.tensor_tensor(y_sb[:, t, :], y3[:, t, :], x_sb[:, TILES - LAST:TILES, :],
                                    ALU.add).then_inc(y_done, 1)

        @block.tensor
        def _(pe):
            mm = nc.tensor.matmul

            def fold_weights():
                pe.wait_ge(keys_in, 16)
                for t in range(2):
                    last = nc.tensor.transpose(f_bank[:, bass.ts(t, P)], keys_sb[:, t, :], ident[:, :])
                last.then_inc(keysT_ready, 1)
                pe.wait_ge(fwq_in, 16 * FWQ_DMAS)
                pe.wait_ge(keysT_out, 1)
                for h in range(HEADS):
                    last = mm(sim_bank[1][:, bass.ts(h, 2 * KEYS)], fwq_sb[:, h, :],
                              keysT[:, h, :, :].rearrange("p s k -> p (s k)"), start=True, stop=True)
                last.then_inc(fold_ready, 1)

            def fill(u, parity, after=None):
                if not (isinstance(u, int) and u < 2):
                    wait_reg(pe, unit_out, u - 1)
                if after is not None:
                    wait_reg(pe, unit_out, after + 1)
                return scratch[parity]

            def transpose_rows(b):
                pe.wait_ge(xn_done[b % 2], b // 2 + 1)
                if b >= 2:
                    pe.wait_ge(xt_out, b - 1)
                for j in range(TB):
                    last = nc.tensor.transpose(scratch[b % 2][:, bass.ts(j, P)], xn_all[:, TB * b + j, :], ident[:, :])
                last.then_inc(xt_full, 1)

            def logits(b):
                pe.wait_ge(xt_out, b + 1)
                return mm(z_bank[0:4 * B, :], zw_rows[:, b, :, :].rearrange("p g r -> p (g r)"),
                          xT_all[:, bass.ts(b, L)], start=(b == 0), stop=(b == B - 1))

            def hidden(b):
                if b >= 2:
                    pe.wait_ge(side_out, b - 1)
                mm(side_bank[b % 2][0:CANDS, :], downT[:, :], xT_all[:, bass.ts(b, L)],
                   start=True, stop=True).then_inc(side_full, 1)

            def scores(n, j, b, first=False):
                if first and n < TB:
                    rows = xT_all[:, bass.ts(n, P)]
                else:
                    pe.wait_ge(tile_in[j], 16 * b)
                    rows = xTc[:, j, :]
                if not (first and n < 2):
                    pe.wait_ge(sim_used, 2 * n - 2)
                mm(sim_bank[j % 2][:, :], rows, sim_w[:, :], start=True, stop=True).then_inc(sim_ready, 1)

            def expert_weights(n, j, first=False):
                d = j % 2
                pe.wait_ge(wgt_done, n + 1)
                for h in range(HEADS):
                    last = mm(c_bank[0:CANDS, bass.ts(j, P)], wgt[d][:, h, :], ident[:, :],
                              start=(h == 0), stop=(h == HEADS - 1))
                last.then_inc(c_ready, 1)

            def experts_out(b, tiles=range(TB), count=1, dst=f_bank):
                pe.wait_ge(act_done, b + count)
                for j in tiles:
                    last = mm(dst[:, bass.ts(j, D)], actT[:, bass.ts(j, P)], up_sb[:, :], start=True, stop=True)
                last.then_inc(f_ready, 1)

            def project_windows(b):
                for k, w in ((U_QW, wq_sb), (U_KW, wk_sb), (U_VW, wv_sb)):
                    o = fill(m_unit(b, k), k % 2)
                    mm(o[:, 0:WTOK], w[:, :], xT_all[:, bass.ds(b * L, WTOK)],
                       start=True, stop=True).then_inc(unit_full, 1)
                o = fill(m_unit(b, U_COMP), U_COMP % 2)
                rows = xT_all[:, bass.ts(b, L)].rearrange("p (c r) -> p r c", r=RATIO)
                for r in range(RATIO):
                    last = mm(o[:, 0:BLOCKS], wc_sb[:, r, :], rows[:, r, :], start=(r == 0), stop=(r == RATIO - 1))
                last.then_inc(unit_full, 1)

            def project_selected(b):
                pe.wait_ge(pick_done, b + 1)
                o = fill(m_unit(b, U_SEL), U_SEL % 2)
                for j in range(TB):
                    last = mm(o[0:SELECT_K, 0:D], pick[:, j, :],
                              xn_all[:, bass.ds(b * TB + j, 1), :].rearrange("p a d -> p (a d)"),
                              start=(j == 0), stop=(j == TB - 1))
                last.then_inc(unit_full, 1)
                o = fill(m_unit(b, U_SELT), U_SELT % 2, m_unit(b, U_SEL))
                nc.tensor.transpose(o[:, 0:SELECT_K], xsel[:, :], ident[0:SELECT_K, 0:SELECT_K]).then_inc(unit_full, 1)
                o = fill(m_unit(b, U_QK), U_QK % 2, m_unit(b, U_SELT))
                mm(o[:, 0:CS], wq_sb[:, :], csT[:, :], start=True, stop=True)
                mm(o[:, CS:2 * CS], wk_sb[:, :], csT[:, :], start=True, stop=True).then_inc(unit_full, 1)
                o = fill(m_unit(b, U_V), U_V % 2)
                mm(o[:, 0:CS], wv_sb[:, :], csT[:, :], start=True, stop=True).then_inc(unit_full, 1)

            def attention_scores(b, first=False):
                pe.wait_ge(unit_out, m_unit(b, U_QK) + 1)
                if first:
                    pe.wait_ge(gate_exp, 1)
                else:
                    pe.wait_ge(p_exp, b)
                mm(s_bank[:, 0:TB * WKEYS], ident[:, :], win_mask[:, :, :].rearrange("p g k -> p (g k)"),
                   start=True, stop=False)
                for g in range(TB):
                    k0 = g * WPT * STEP_W
                    mm(s_bank[:, bass.ts(g, WKEYS)], qw[:, bass.ts(g, P)], kw[:, k0:k0 + WKEYS],
                       start=False, stop=(g == TB - 1))
                c0 = TB * WKEYS
                mm(s_bank[:, c0:c0 + BLOCKS], qcs[:, 0:BLOCKS], kcs[:, 0:BLOCKS], start=True, stop=True)
                mm(s_bank[0:SELECT_K, c0 + BLOCKS:c0 + CS], qcs[:, BLOCKS:CS], kcs[:, BLOCKS:CS],
                   start=True, stop=True).then_inc(s_ready, 1)

            def values_out(b):
                o = fill(m_unit(b, U_VWW), U_VWW % 2, m_unit(b, U_V))
                for g in range(TB):
                    k0 = g * WPT * STEP_W
                    last = mm(o[0:WKEYS, bass.ts(g, D)], vw[:, k0:k0 + WKEYS], wo_sb[:, WIN, :], start=True, stop=True)
                last.then_inc(unit_full, 1)
                o = fill(m_unit(b, U_VWC), U_VWC % 2)
                mm(o[:, 0:D], vcs[:, 0:BLOCKS], wo_sb[:, COMP, :], start=True, stop=True)
                mm(o[0:SELECT_K, D:2 * D], vcs[:, BLOCKS:CS], wo_sb[:, SEL, :], start=True, stop=True).then_inc(unit_full, 1)

            def attention_out(b, first=False):
                pe.wait_ge(p_scaled, b + 1)
                o = fill(m_unit(b, U_PTW), U_PTW % 2)
                for g in range(TB):
                    last = nc.tensor.transpose(o[0:WKEYS, bass.ts(g, P)], p_win[:, g, :], ident[:, :])
                last.then_inc(unit_full, 1)
                o = fill(m_unit(b, U_PTC), U_PTC % 2)
                nc.tensor.transpose(o[:, 0:P], p_cs[:, 0:BLOCKS], ident[:, :])
                nc.tensor.transpose(o[0:SELECT_K, P:P + SELECT_K], p_cs[0:SELECT_K, BLOCKS:CS],
                                    ident[0:SELECT_K, 0:SELECT_K]).then_inc(unit_full, 1)
                pe.wait_ge(unit_out, m_unit(b, U_PTC) + 1)
                if not first:
                    pe.wait_ge(s_done, b)
                for j in range(TB):
                    o = out_bank[:, bass.ts(j, D)]
                    mm(o, ident[:, :], xn_all[:, bass.ds(b * TB + j, 1), :].rearrange("p a d -> p (a d)"),
                       start=True, stop=False)
                    if j == 0:
                        mm(o, pT_cs[:, 0, :], vwc[:, 0, :], start=False, stop=False)
                        mm(o, pT_cs[0:SELECT_K, 1, :], vwc[0:SELECT_K, 1, :], start=False, stop=False)
                    last = mm(o, pT_win[:, j, :], vww[:, j, :], start=False, stop=True)
                last.then_inc(out_ready, 1)

            def body(b, first=False, last=False):
                for j in range(TB):
                    n = TB * b + j
                    if first and j == 0:
                        scores(3, 3, 0, True)
                    if not (last and j == TB - 1) and not (first and j < TB - 1):
                        scores(n + 1, (j + 1) % TB, b + (j + 1) // TB, first)
                    if j == 0:
                        project_windows(b)
                    if j == 1:
                        if first:
                            pe.wait_ge(rank_out, 1)
                            for t in range(TB):
                                rank_t = nc.tensor.transpose(f_bank[:, bass.ts(t, B)], sel_rank[:, bass.ts(t, P)],
                                                             ident[0:B, 0:B])
                            rank_t.then_inc(rankT_ready, 1)
                        project_selected(b)
                        attention_scores(b, first)
                    if j == 2:
                        values_out(b)
                        if not first:
                            experts_out(b - 1)
                    if first and j == 3:
                        expert_weights(1, 1, True)
                    if j == 3:
                        attention_out(b, first)
                    if not (first and j != 2):
                        if j == 2 and not first:
                            pe.wait_ge(c_out, b)
                        expert_weights(n - 2, (j + 2) % TB, first)

            pe.wait_ge(consts, CONSTS)
            fold_weights()
            transpose_rows(0)
            pe.wait_ge(xt_out, 1)
            pe.wait_ge(sim_w_done, 1)
            scores(0, 0, 0, True)
            transpose_rows(1)
            pe.wait_ge(zw_done, 1)
            for b in range(B):
                last = logits(b)
                if b == 0:
                    scores(1, 1, 0, True)
                if b + 2 < B:
                    transpose_rows(b + 2)
            last.then_inc(z_ready, 1)
            scores(2, 2, 0, True)
            pe.wait_ge(down_in, 16 * DOWN_DMAS)
            nc.tensor.transpose(c_bank[:, 0:CANDS], down_sb[:, :], ident[0:CANDS, 0:CANDS]).then_inc(downT_ready, 1)
            pe.wait_ge(downT_out, 1)
            for b in range(B):
                if b == 1:
                    pe.wait_ge(z_done, 1)
                    for t in range(TB):
                        last = nc.tensor.transpose(z_bank[:, bass.ts(t, 4 * B)], z_sb[:, bass.ts(t, P)],
                                                   ident[0:4 * B, 0:4 * B])
                    last.then_inc(gate_ready, 1)
                hidden(b)
            pe.wait_ge(w_late, 16 * LATE_DMAS)
            body(0, first=True)
            with pe.Fori(1, B - 1) as b:
                body(b)
            body(B - 1, last=True)
            experts_out(B - 1, range(TB - LAST))
            for k in range(LAST):
                pe.wait_ge(head_sum, k + 1)
                nc.tensor.transpose(last_c[0:CANDS, bass.ts(k, P)], wsum[:, k, :], ident[:, :]).then_inc(c_ready, 1)
            experts_out(B - 1, range(TB - LAST, TB), 2, dst=last_f)


_INS = ["L0_attn_hidden_states", "L0_attn_Wq", "L0_attn_bq", "L0_attn_Wk", "L0_attn_bk", "L0_attn_Wv",
        "L0_attn_bv", "L0_attn_Wo", "L0_attn_bo", "L0_attn_Wg", "L0_attn_bg", "L0_attn_Wc", "L0_attn_bc",
        "L0_attn_Ws", "L0_attn_bs", "L0_ffn_Wq", "L0_ffn_keys", "L0_ffn_W_down", "L0_ffn_W_up"]


def kernel(**inputs):
    import numpy as np
    import concourse.bacc as bacc
    from concourse.bass_utils import run_bass_kernel_spmd

    nc = bacc.Bacc("TRN2", target_bir_lowering=False, num_devices=1)
    arrays, args = {}, []
    for name in _INS:
        a = np.ascontiguousarray(inputs[name])
        arrays[f"in_{name}"] = a
        args.append(nc.dram_tensor(f"in_{name}", a.shape, mybir.dt.from_np(a.dtype), kind="ExternalInput").ap())
    shape = inputs["L0_attn_hidden_states"].shape
    args.append(nc.dram_tensor("out_0", shape, F32, kind="ExternalOutput").ap())
    program(nc, *args)
    r = run_bass_kernel_spmd(nc, [arrays], core_ids=[0])
    return r.results[0]["out_0"]
```
